# Optimizing a Trainium2 kernel written in Bass

```python
import numpy as np
import jax
import jax.numpy as jnp

def _softmax(x, axis=-1):
    return jax.nn.softmax(x, axis=axis)

def _gelu(x):
    return jax.nn.gelu(x, approximate=True)

def _silu(x):
    return jax.nn.silu(x)

def _sigmoid(x):
    return jax.nn.sigmoid(x)

def _layernorm(x, axis=-1, eps=1e-05):
    m = jnp.mean(x, axis=axis, keepdims=True)
    v = jnp.var(x, axis=axis, keepdims=True)
    return (x - m) / jnp.sqrt(v + eps)

def _scatter_add(tgt, idx, src, axis=0):
    return tgt.at[idx].add(src)

def _segment_sum(src, seg, n):
    return jax.ops.segment_sum(src, seg, n)
kernel_name = 'mk_prb_d1_jaxref_r8_7908f4'

def setup_inputs(seed: int=0):
    np.random.seed(seed)
    _w = jnp.asarray

    def _L0_attn_setup():
        import jax, jax.numpy as jnp
        import numpy as np
        EPS = 1e-06
        N_HEADS = 16

        def _stable_softmax(x):
            x_max = jax.lax.stop_gradient(jnp.max(x, axis=-1, keepdims=True))
            exp_x = jnp.exp(jnp.clip(x - x_max, -50.0, 50.0))
            return exp_x / (jnp.sum(exp_x, axis=-1, keepdims=True) + EPS)
        key = jax.random.key(seed)
        k1, k2, k3 = jax.random.split(key, 3)
        B, S, D = (2, 256, 128)
        x = jax.random.normal(k1, (B, S, D), dtype=jnp.float32)
        Wqkv = jax.random.normal(k2, (3 * D, D), dtype=jnp.float32) * 0.02
        Wout = jax.random.normal(k3, (D, D), dtype=jnp.float32) * (0.02 / np.sqrt(2))
        return {'x': x, 'Wqkv': Wqkv, 'Wout': Wout}
    _L0_attn_in = _L0_attn_setup()

    def _L0_ffn_setup():
        import jax, jax.numpy as jnp
        import numpy as np
        D = 128
        H = 16
        DH = D // H
        DC = D // 4
        HID = 256
        G = 2
        EPG = 4
        E = G * EPG
        TOPK = 2
        EPS = 1e-06
        B, T = (2, 256)

        def _rope_sincos(t, dh):
            inv_freq = 1.0 / 10000.0 ** (jnp.arange(0, dh, 2, dtype=jnp.float32) / dh)
            ang = jnp.arange(t, dtype=jnp.float32)[:, None] * inv_freq[None, :]
            return (jnp.sin(ang), jnp.cos(ang))

        def _apply_rope(x, sin, cos):
            x1 = x[..., ::2]
            x2 = x[..., 1::2]
            r = jnp.stack([x1 * cos - x2 * sin, x1 * sin + x2 * cos], axis=-1)
            return r.reshape(x.shape)

        def _swiglu(x):
            a, b = jnp.split(x, 2, axis=-1)
            return jax.nn.silu(a) * b

        def _rmsnorm(x, w):
            return x * jax.lax.rsqrt(jnp.mean(x * x, axis=-1, keepdims=True) + EPS) * w
        key = jax.random.key(seed)
        ks = jax.random.split(key, 14)
        s = 0.02
        return {'src': jax.random.normal(ks[0], (B, T, D), jnp.float32), 'Wq': jax.random.normal(ks[1], (D, D), jnp.float32) * s, 'Wk_c': jax.random.normal(ks[2], (D, DC), jnp.float32) * s, 'Wv_c': jax.random.normal(ks[3], (D, DC), jnp.float32) * s, 'Wk': jax.random.normal(ks[4], (DC, D), jnp.float32) * s, 'Wv': jax.random.normal(ks[5], (DC, D), jnp.float32) * s, 'Wo': jax.random.normal(ks[6], (D, D), jnp.float32) * s, 'W_shared_in': jax.random.normal(ks[7], (D, 2 * HID), jnp.float32) * s, 'W_shared_out': jax.random.normal(ks[8], (HID, D), jnp.float32) * s, 'W1_shared': jax.random.normal(ks[9], (D, 2 * HID), jnp.float32) * s, 'W2_experts': jax.random.normal(ks[10], (E, HID, D), jnp.float32) * s, 'Wg_gate': jax.random.normal(ks[11], (D, G), jnp.float32) * s, 'We_gate': jax.random.normal(ks[12], (D, E), jnp.float32) * s, 'group_bias': jnp.zeros((G,), jnp.float32), 'expert_bias': jnp.zeros((E,), jnp.float32), 'norm1_w': jnp.ones((D,), jnp.float32), 'norm2_w': jnp.ones((D,), jnp.float32)}
    _L0_ffn_in = _L0_ffn_setup()
    _d = {'L0_attn_x': _L0_attn_in['x'], 'L0_attn_Wqkv': _L0_attn_in['Wqkv'], 'L0_attn_Wout': _L0_attn_in['Wout'], 'L0_ffn_Wq': _L0_ffn_in['Wq'], 'L0_ffn_Wk_c': _L0_ffn_in['Wk_c'], 'L0_ffn_Wv_c': _L0_ffn_in['Wv_c'], 'L0_ffn_Wk': _L0_ffn_in['Wk'], 'L0_ffn_Wv': _L0_ffn_in['Wv'], 'L0_ffn_Wo': _L0_ffn_in['Wo'], 'L0_ffn_W_shared_in': _L0_ffn_in['W_shared_in'], 'L0_ffn_W_shared_out': _L0_ffn_in['W_shared_out'], 'L0_ffn_W1_shared': _L0_ffn_in['W1_shared'], 'L0_ffn_W2_experts': _L0_ffn_in['W2_experts'], 'L0_ffn_Wg_gate': _L0_ffn_in['Wg_gate'], 'L0_ffn_We_gate': _L0_ffn_in['We_gate'], 'L0_ffn_group_bias': _L0_ffn_in['group_bias'], 'L0_ffn_expert_bias': _L0_ffn_in['expert_bias'], 'L0_ffn_norm1_w': _L0_ffn_in['norm1_w'], 'L0_ffn_norm2_w': _L0_ffn_in['norm2_w']}
    _x0 = _d['L0_attn_x']
    _d['L0_attn_x'] = jax.random.normal(jax.random.fold_in(jax.random.key(seed), 1), (16, 512, 128), dtype=_x0.dtype)
    del _x0
    return _d

def reference(L0_attn_x, L0_attn_Wqkv, L0_attn_Wout, L0_ffn_Wq, L0_ffn_Wk_c, L0_ffn_Wv_c, L0_ffn_Wk, L0_ffn_Wv, L0_ffn_Wo, L0_ffn_W_shared_in, L0_ffn_W_shared_out, L0_ffn_W1_shared, L0_ffn_W2_experts, L0_ffn_Wg_gate, L0_ffn_We_gate, L0_ffn_group_bias, L0_ffn_expert_bias, L0_ffn_norm1_w, L0_ffn_norm2_w):

    def _L0_attn_ref(x, Wqkv, Wout):
        import jax, jax.numpy as jnp
        import numpy as np
        EPS = 1e-06
        N_HEADS = 16

        def _stable_softmax(x):
            x_max = jax.lax.stop_gradient(jnp.max(x, axis=-1, keepdims=True))
            exp_x = jnp.exp(jnp.clip(x - x_max, -50.0, 50.0))
            return exp_x / (jnp.sum(exp_x, axis=-1, keepdims=True) + EPS)
        B, S, D = x.shape
        H = N_HEADS
        Dh = D // H
        scale = 1.0 / np.sqrt(Dh)
        qkv = (x @ Wqkv.T).reshape(B, S, 3, H, Dh)
        qkv = jnp.transpose(qkv, (2, 0, 3, 1, 4))
        q, k, v = (qkv[0], qkv[1], qkv[2])
        scores = jnp.einsum('bhqd,bhkd->bhqk', q, k) * scale
        attn = _stable_softmax(scores)
        out = jnp.einsum('bhqk,bhkd->bhqd', attn, v)
        out = jnp.transpose(out, (0, 2, 1, 3)).reshape(B, S, D)
        return out @ Wout.T

    def _L0_ffn_ref(src, Wq, Wk_c, Wv_c, Wk, Wv, Wo, W_shared_in, W_shared_out, W1_shared, W2_experts, Wg_gate, We_gate, group_bias, expert_bias, norm1_w, norm2_w):
        import jax, jax.numpy as jnp
        import numpy as np
        D = 128
        H = 16
        DH = D // H
        DC = D // 4
        HID = 256
        G = 2
        EPG = 4
        E = G * EPG
        TOPK = 2
        EPS = 1e-06
        B, T = (2, 256)

        def _rope_sincos(t, dh):
            inv_freq = 1.0 / 10000.0 ** (jnp.arange(0, dh, 2, dtype=jnp.float32) / dh)
            ang = jnp.arange(t, dtype=jnp.float32)[:, None] * inv_freq[None, :]
            return (jnp.sin(ang), jnp.cos(ang))

        def _apply_rope(x, sin, cos):
            x1 = x[..., ::2]
            x2 = x[..., 1::2]
            r = jnp.stack([x1 * cos - x2 * sin, x1 * sin + x2 * cos], axis=-1)
            return r.reshape(x.shape)

        def _swiglu(x):
            a, b = jnp.split(x, 2, axis=-1)
            return jax.nn.silu(a) * b

        def _rmsnorm(x, w):
            return x * jax.lax.rsqrt(jnp.mean(x * x, axis=-1, keepdims=True) + EPS) * w
        Bb, Tt, C = src.shape
        q = (src @ Wq).reshape(Bb, Tt, H, DH).transpose(0, 2, 1, 3)
        k = (src @ Wk_c @ Wk).reshape(Bb, Tt, H, DH).transpose(0, 2, 1, 3)
        v = (src @ Wv_c @ Wv).reshape(Bb, Tt, H, DH).transpose(0, 2, 1, 3)
        sin, cos = _rope_sincos(Tt, DH)
        q = _apply_rope(q, sin, cos)
        k = _apply_rope(k, sin, cos)
        attn = jnp.einsum('bhqd,bhkd->bhqk', q, k) / np.sqrt(DH).astype(np.float32)
        attn = jax.nn.softmax(attn, axis=-1)
        sa = jnp.einsum('bhqk,bhkd->bhqd', attn, v)
        sa = sa.transpose(0, 2, 1, 3).reshape(Bb, Tt, C) @ Wo
        x = _rmsnorm(src + sa, norm1_w)
        S = Bb * Tt
        flat = x.reshape(S, C)
        shared = _swiglu(flat @ W_shared_in) @ W_shared_out
        g_probs = jax.nn.softmax(flat @ Wg_gate + group_bias, -1)
        g_idx = jnp.argmax(g_probs, axis=-1)
        e_logits = flat @ We_gate + expert_bias
        e_group = jnp.arange(E) // EPG
        in_group = e_group[None, :] == g_idx[:, None]
        e_probs = jax.nn.softmax(jnp.where(in_group, e_logits, -jnp.inf), -1)
        g_prob = jnp.take_along_axis(g_probs, g_idx[:, None], axis=1)
        p_expert = e_probs * g_prob
        topv, topi = jax.lax.top_k(p_expert, TOPK)
        w = jnp.zeros((S, E), flat.dtype).at[jnp.arange(S)[:, None], topi].set(topv)
        h = _swiglu(flat @ W1_shared)
        routed = jnp.zeros_like(shared)
        for e in range(E):
            routed = routed + h @ W2_experts[e] * w[:, e:e + 1]
        out = x + (shared + routed).reshape(Bb, Tt, C)
        return _rmsnorm(out, norm2_w)
    x = L0_attn_x
    xn = _layernorm(x, axis=-1)
    x = x + _L0_attn_ref(xn, L0_attn_Wqkv, L0_attn_Wout) + _L0_ffn_ref(xn, L0_ffn_Wq, L0_ffn_Wk_c, L0_ffn_Wv_c, L0_ffn_Wk, L0_ffn_Wv, L0_ffn_Wo, L0_ffn_W_shared_in, L0_ffn_W_shared_out, L0_ffn_W1_shared, L0_ffn_W2_experts, L0_ffn_Wg_gate, L0_ffn_We_gate, L0_ffn_group_bias, L0_ffn_expert_bias, L0_ffn_norm1_w, L0_ffn_norm2_w)
    return x

_drawn_inputs = setup_inputs


def setup_inputs(seed=0):
    import zlib

    import numpy as np

    out = dict(_drawn_inputs(seed))
    spreads = {'L0_ffn_group_bias': (0.0, 0.8),
     'L0_ffn_expert_bias': (0.0, 0.8),
     'L0_ffn_norm1_w': (1.0, 0.2),
     'L0_ffn_norm2_w': (1.0, 0.2)}
    factors = {'L0_attn_Wqkv': 8.0,
     'L0_attn_Wout': 8.0,
     'L0_ffn_Wq': 8.0,
     'L0_ffn_Wk_c': 8.0,
     'L0_ffn_Wv_c': 8.0,
     'L0_ffn_Wk': 8.0,
     'L0_ffn_Wv': 8.0,
     'L0_ffn_Wo': 8.0,
     'L0_ffn_W_shared_in': 8.0,
     'L0_ffn_W_shared_out': 8.0,
     'L0_ffn_W1_shared': 8.0,
     'L0_ffn_W2_experts': 8.0,
     'L0_ffn_Wg_gate': 8.0,
     'L0_ffn_We_gate': 8.0}
    for name, (base, spread) in spreads.items():
        noise = np.random.default_rng([zlib.crc32(name.encode()), seed]).standard_normal(out[name].shape)
        drawn = base * np.exp(spread * noise) if base else spread * noise
        out[name] = jnp.asarray(drawn.astype(out[name].dtype))
    for name, factor in factors.items():
        out[name] = (out[name] * factor).astype(out[name].dtype)
    return out
```

```python
from contextlib import ExitStack

import numpy as np

import concourse.bass as bass
from concourse import mybir

ALU = mybir.AluOpType
ACT = mybir.ActivationFunctionType
AX = mybir.AxisListType
F32 = mybir.dt.float32
BF16 = mybir.dt.bfloat16

B, S, D = 16, 512, 128
H, DH = 16, 8
NT = S // 128
HID = 256
E, G, EPG = 8, 2, 4
NL = G + E
TERMS = 6
ROWS = TERMS * 2 * DH
MROWS = 6
Q_PART = [0, 1, 0, 1, 2, 0]
K_PART = [0, 0, 1, 1, 0, 2]
SLOTS, QUARTERS = H, 4
VALUE_AT = 1
UNIT = H * NT
SCALE = float(1.0 / np.sqrt(DH))
FLOOR = float(np.exp(np.float32(-50.0)))
EPS_DEN, EPS_LN, EPS_RMS = 1e-6, 1e-5, 1e-6
PLAIN, ROPE = 0, 1
QK_DMAS = TERMS * 3
VW = 48

EVEN = [("shared_out", [3, 5]), ("max_rope1", [7]), ("exp0", [9, 11]), ("exp1", [13, 15]),
        ("o_plain1", [20]), ("back_plain", [23]), ("y_plain", [26]), ("exp2", [28, 30]),
        ("exp3", [32, 34]), ("exp4", [36, 38]), ("max_plain0", [40]), ("exp5", [43, 45]),
        ("o_rope0", [52]), ("exp6", [53, 55]), ("exp7", [57, 59])]
ODD = [("xnT", [2]), ("q_plain", [4]), ("max_plain1", [7]), ("k_plain", [10]), ("o_rope1", [20]),
       ("back_rope", [23]), ("y_rope", [26]), ("q_rope", [28]), ("qs_rope", [30]), ("k_rope", [32]),
       ("ks_rope", [34]), ("x1T", [36]), ("max_rope0", [38]), ("gates", [40]), ("up0", [42]),
       ("down0", [44]), ("up1", [46]), ("v0", [47]), ("o_plain0", [52]), ("down1", [53]),
       ("up2", [54]), ("down2", [56]), ("up3", [58]), ("down3", [60]), ("v1", [62])]
TABLE = {"even": EVEN, "odd": ODD}
LAG = {"max_rope1": -1, "shared_out": -2, "o_plain1": -1, "back_plain": -1, "y_plain": -1,
       "max_plain0": 0, "o_rope0": -1, "max_plain1": 0, "xnT": 1, "q_plain": 1, "k_plain": 1,
       "o_rope1": -1, "back_rope": -1, "y_rope": -1, "q_rope": 1, "qs_rope": 1, "k_rope": 1,
       "ks_rope": 1, "x1T": -1, "max_rope0": 0, "gates": -1, "v0": 1, "v1": 1, "o_plain0": 0}
LAG |= {f"exp{n}": -2 for n in range(8)}
LAG |= {f"{w}{n}": -1 for n in range(4) for w in ("up", "down")}
ORDER = [name for name, _ in EVEN + ODD]
FIRST_LOOP, LAST_LOOP = 2, B - 2


def live(b, lag):
    return not isinstance(b, int) or 0 <= b + lag < B


def side_bank(job):
    return ORDER.index(job) % 2


def side_uses(b, job):
    bank, at = side_bank(job), ORDER.index(job)
    same = [n for n in ORDER if side_bank(n) == bank]
    before = [n for n in same if ORDER.index(n) < at]
    if not isinstance(b, int):
        head = sum(live(c, LAG[n]) for c in range(-1, FIRST_LOOP) for n in same)
        return (b + (-FIRST_LOOP)) * len(same) + (head + len(before))
    return sum(live(c, LAG[n]) for c in range(-1, b) for n in same) + sum(live(b, LAG[n]) for n in before)


def cnt(b, lag, per, k):
    return b * per + (lag * per + k)


def need(eng, semaphore, value):
    if not isinstance(value, int) or value > 0:
        eng.wait_ge(semaphore, value)


def after(step, job, quarters=1):
    return dict(TABLE[step])[job][-1] + quarters


def jobs_at(step, t):
    return [(name, at.index(t)) for name, at in TABLE[step] if t in at]


def layer_kernel(nc, x, wq, wkcT, wk, wvcT, wvp, wvr, wo, w_up, w_out, w2, w_gate, bias, norms, consts, out):
    ctx = ExitStack()
    with ctx:
        def sb(name, shape, dt=F32):
            return ctx.enter_context(nc.sbuf_tensor(name, shape, dt))

        def sem(name):
            return ctx.enter_context(nc.semaphore(name))

        score_ps = ctx.enter_context(nc.psum_tensor("score_ps", [128, 3, 512], F32))
        shift_ps = ctx.enter_context(nc.psum_tensor("shift_ps", [128, 2, 512], F32))
        o_ps = ctx.enter_context(nc.psum_tensor("o_ps", [128, 512], F32))
        side_ps = ctx.enter_context(nc.psum_tensor("side_ps", [128, 2, 512], F32))

        wq_sb = sb("wq_sb", [128, 4, 128])
        wkr_sb = sb("wkr_sb", [128, 2, 128])
        wv_sb = sb("wv_sb", [128, 2, 128])
        wo_sb = sb("wo_sb", [128, 2, 128])
        w_up_sb = sb("w_up_sb", [128, 8, 128])
        w_out_sb = sb("w_out_sb", [128, 2, 128])
        w2_sb = sb("w2_sb", [128, 2, E * 128])
        w_gate_sb = sb("w_gate_sb", [128, NL])
        bias_sb = sb("bias_sb", [128, NL])
        norm_sb = sb("norm_sb", [128, 2, 128])
        const_sb = sb("const_sb", [128, 128 + 2 * S])
        ident = const_sb[:, 0:128]
        cos = const_sb[:, 128:128 + S]
        sin = const_sb[:, 128 + S:128 + 2 * S]
        ident_bf = sb("ident_bf", [128, 128], BF16)
        minus_half = sb("minus_half", [128, NT])
        rank0 = sb("rank0", [128, NT, EPG])

        qt = [sb(f"qt{a}", [ROWS + MROWS, H // 2, S], BF16) for a in range(2)]
        kt = [sb(f"kt{a}", [ROWS + MROWS, H, S], BF16) for a in range(2)]
        vt = [sb(f"vt{a}", [128, NT, H // 2, VW]) for a in range(2)]
        v_stage = sb("v_stage", [128, NT, 2, 128])
        q_parts = [sb(f"q_parts{a}", [128, 3, S], BF16) for a in range(2)]
        k_parts = [sb(f"k_parts{a}", [128, 3, S], BF16) for a in range(2)]
        q_rest = sb("q_rest", [128, S])
        k_rest = sb("k_rest", [128, S])
        roped = sb("roped", [128, 2, S])
        turned = sb("turned", [128, S])
        weights = sb("weights", [128, 8, NT, S])
        factors = weights[0:32, 0, :, :].rearrange("p t n -> p (t n)")
        wkcT_sb, wvcT_sb, wvr_sb = (factors[:, 128 * n:128 * n + 128] for n in range(3))
        wk_sb = factors[:, 384:640].rearrange("p (a n) -> p a n", a=2)
        negmax = sb("negmax", [128, 2, NT, 8])
        max_rest = sb("max_rest", [128, NT, 8])
        max_parts = sb("max_parts", [128, 2, NT, 24], BF16)
        max_rows = sb("max_rows", [24, 2, S], BF16)
        o_sb = sb("o_sb", [128, S])
        den = sb("den", [128, NT, 8])
        inv_den = sb("inv_den", [128, NT, 8])
        heads = [sb(f"heads{a}", [128, NT, 128]) for a in range(2)]
        headsT = sb("headsT", [128, S])

        x_in = sb("x_in", [128, NT, 128])
        stats = sb("stats", [128, NT, 6])
        moments = sb("moments", [128, NT, 2])
        ln_var = sb("ln_var", [128, NT])
        ln_rstd = sb("ln_rstd", [128, NT])
        xn_new = sb("xn_new", [128, NT, 128])
        xn_mid = sb("xn_mid", [128, NT, 128])
        xn_old = sb("xn_old", [128, NT, 128])
        xnT = sb("xnT", [128, S])
        res_new = sb("res_new", [128, NT, 128])
        res_old = sb("res_old", [128, NT, 128])
        x1 = sb("x1", [128, NT, 128])
        out_sb = sb("out_sb", [128, NT, 128])
        sums = sb("sums", [128, 2, NT])
        rms = sb("rms", [128, 2, NT])
        x1T = sb("x1T", [128, S])
        tanh = sb("tanh", [128, S])
        square = tanh[:, :].rearrange("p (t c) -> p t c", t=NT)
        spread = sb("spread", [128, 2, 4, 128])
        two = sb("two", [128, 2, 128])
        one = sb("one", [128, 128])
        hidden = sb("hidden", [128, 4, S])
        logits = sb("logits", [128, NT, NL])
        in_group = sb("in_group", [128, 2, NT, 1])
        gap = sb("gap", [128, NT, 1])
        low = sb("low", [128, NT, 1])
        sel0 = sb("sel0", [128, NT, EPG])
        sel1 = sb("sel1", [128, NT, EPG])
        top = sb("top", [128, NT, 1])
        z = sb("z", [128, NT, 1 + EPG])
        ez = sb("ez", [128, NT, 1 + EPG])
        total = sb("total", [128, NT, 2])
        share = sb("share", [128, NT, 2])
        prob = sb("prob", [128, NT, EPG])
        above = [sb(f"above{s}", [128, NT, EPG - s]) for s in range(1, EPG)]
        rank = sb("rank", [128, NT, EPG])
        gate = sb("gate", [128, NT, E])

        loaded = sem("loaded")
        kt_made = sem("kt_made")
        ready = sem("ready")
        passed = sem("passed")
        product = sem("product")
        merged = sem("merged")
        x_landed = sem("x_landed")
        stats_done = sem("stats_done")
        moments_done = sem("moments_done")
        var_done = sem("var_done")
        rstd_done = sem("rstd_done")
        xn_done = sem("xn_done")
        mid_landed = sem("mid_landed")
        old_landed = sem("old_landed")
        hi_done = [sem("hi_plain"), sem("hi_rope")]
        mid_done = [sem("mid_plain"), sem("mid_rope")]
        lo_done = [sem("lo_plain"), sem("lo_rope")]
        rope_done = sem("rope_done")
        rope_rest = sem("rope_rest")
        v_placed = [sem("v_plain"), sem("v_rope")]
        qk_landed = [[sem(f"qk{a}{g}") for g in range(2)] for a in range(2)]
        scored = sem("scored")
        max_taken = sem("max_taken")
        max_hi = sem("max_hi")
        max_r = sem("max_r")
        max_mid = sem("max_mid")
        max_split = sem("max_split")
        max_landed = [sem("max_plain"), sem("max_rope")]
        shifted = sem("shifted")
        weighed = sem("weighed")
        clip_dve = sem("clip_dve")
        clip_pool = sem("clip_pool")
        valued = sem("valued")
        o_copied = sem("o_copied")
        den_done = sem("den_done")
        inv_done = sem("inv_done")
        res_landed = sem("res_landed")
        res_moved = sem("res_moved")
        squared = sem("squared")
        summed = sem("summed")
        mean_done = sem("mean_done")
        rms_done = sem("rms_done")
        x1_done = sem("x1_done")
        route = sem("route")
        top_done = sem("top_done")
        z_exp = sem("z_exp")
        shares_done = sem("shares_done")
        tanh_done = sem("tanh_done")
        mixed = sem("mixed")
        scaled = sem("scaled")
        final_done = sem("final_done")
        stored = sem("stored")
        side_full = [sem("side_full0"), sem("side_full1")]
        side_free = [sem("side_free0"), sem("side_free1")]

        LOADS = ((wkcT_sb, wkcT), (wk_sb, wk), (wvcT_sb, wvcT), (wvr_sb, wvr),
                 (const_sb[:], consts), (wq_sb[:], wq), (wv_sb[:, 0, :], wvp), (wo_sb[:], wo), (w_up_sb[:], w_up),
                 (w_out_sb[:], w_out), (w2_sb[:], w2), (w_gate_sb[:], w_gate),
                 (bias_sb[:], bias[0].partition_broadcast(128)), (norm_sb[:], norms[0].partition_broadcast(128)))
        READY = 7
        ROUTE_A, ROUTE_B = 9, 19
        QK_ALL = 16 * QK_DMAS

        def stand(eng):
            eng.sem_inc(passed, 1)

        def full(eng, b, job):
            eng.wait_ge(side_full[side_bank(job)], side_uses(b, job) + 1)

        def free(job):
            return side_free[side_bank(job)]

        def taken(eng, b, job):
            if live(b, LAG[job]):
                eng.wait_ge(side_free[side_bank(job)], side_uses(b, job) + 1)

        def bank(job):
            return side_ps[:, side_bank(job), :]

        def tiles(ap):
            return ap.rearrange("p (t c) -> p t c", t=NT)

        def norms_done(b, lag, which):
            if isinstance(b, int):
                n = sum(live(c, -2) + live(c, -1) for c in range(-1, b))
                return n + (live(b, -2) if which == 0 else 0)
            head = sum(live(c, -2) + live(c, -1) for c in range(-1, FIRST_LOOP))
            return (b + (-FIRST_LOOP)) * 2 + (head + (1 if which == 0 else 0))

        def all_steps(eng, even, odd):
            for b in range(-1, FIRST_LOOP):
                even(b)
                odd(b)
            with eng.Fori(FIRST_LOOP, LAST_LOOP + 1) as b:
                even(b)
                odd(b)
            for b in range(LAST_LOOP + 1, B + 2):
                even(b)
                odd(b)

        block = ctx.enter_context(nc.Block())

        @block.sync
        def _(sp):
            for dst, src in LOADS:
                sp.dma_start(dst, src).then_inc(loaded, 16)

            def hold(semaphore, value):
                if not isinstance(value, int) or value > 0:
                    sp.wait_ge(semaphore, value)
                    stand(sp)

            def place_qk(b, lag, a, gh):
                if not live(b, lag):
                    return
                for s in (hi_done[a], mid_done[a], lo_done[a]):
                    hold(s, cnt(b, lag, 2, 2))
                if not isinstance(b, int) or b + lag > 0:
                    hold(shifted, cnt(b, lag - 1, 2 * UNIT, UNIT * a + UNIT // 2 * (gh + 1)))
                for t in range(TERMS):
                    sp.dma_start(qt[a][16 * t:16 * t + 16, 4 * gh:4 * gh + 4, :],
                                 q_parts[a][64 * gh:64 * gh + 64, Q_PART[t], :]).then_inc(qk_landed[a][gh], 16)
                    for ab in range(2):
                        row, i, p = 16 * t + 8 * ab, 8 * gh + 4 * ab, 64 * gh + 32 * ab
                        sp.dma_start(kt[a][row:row + 8, i:i + 4, :],
                                     k_parts[a][p:p + 32, K_PART[t], :]).then_inc(qk_landed[a][gh], 16)

            def place_max(b, job):
                lag, a, gh = LAG[job], int(job[4:-1] == "rope"), int(job[-1])
                if live(b, lag):
                    taken(sp, b, job)
                    stand(sp)
                    sp.dma_start(qt[a][ROWS:ROWS + MROWS, 4 * gh:4 * gh + 4, :],
                                 max_rows[:, gh, :]).then_inc(max_landed[a], 16)

            def even(b):
                if live(b, -1):
                    hold(res_moved, cnt(b, -1, 16, 0))
                    sp.dma_start(res_new[:], x[b + (-1)]).then_inc(res_landed, 16)
                place_qk(b, 0, PLAIN, 1)
                place_max(b, "max_rope1")
                if live(b, -1):
                    taken(sp, b + (-1), "y_rope")
                    stand(sp)
                    hold(mid_landed, cnt(b, -1, 16, 16))
                    sp.dma_start(xn_old[:], xn_mid[:]).then_inc(old_landed, 16)
                if live(b, 0):
                    hold(old_landed, cnt(b, -1, 16, 16))
                    hold(xn_done, cnt(b, 0, NT, NT))
                    sp.dma_start(xn_mid[:], xn_new[:]).then_inc(mid_landed, 16)
                if live(b, 1):
                    hold(xn_done, cnt(b, 1, NT, 0))
                    sp.dma_start(x_in[:], x[b + 1]).then_inc(x_landed, 16)
                place_qk(b, 0, ROPE, 0)
                place_max(b, "max_plain0")

            def odd(b):
                place_qk(b, 0, ROPE, 1)
                place_max(b, "max_plain1")
                if live(b, -2):
                    hold(final_done, cnt(b, -2, 1, 1))
                    sp.dma_start(out[b + (-2)], out_sb[:]).then_inc(stored, 16)
                if live(b, -1):
                    taken(sp, b, "y_plain")
                    stand(sp)
                    hold(final_done, cnt(b, -1, 1, 0))
                    sp.dma_start(res_old[:], res_new[:]).then_inc(res_moved, 16)
                place_qk(b, 1, PLAIN, 0)
                place_max(b, "max_rope0")

            all_steps(sp, even, odd)
            sp.wait_ge(stored, 16 * B)

        @block.tensor
        def _(pe):
            pe.wait_ge(loaded, 16 * len(LOADS))
            pe.wait_ge(kt_made, 15)
            pe.wait_ge(ready, READY)
            pe.matmul(side_ps[:, 0, 0:128], wkcT_sb[:, :], wk_sb[:, 0, :], start=True, stop=True)
            pe.matmul(side_ps[:, 0, 128:256], wkcT_sb[:, :], wk_sb[:, 1, :], start=True, stop=True)
            pe.matmul(side_ps[:, 0, 256:384], wvcT_sb[:, :], wvr_sb[:, :], start=True, stop=True).then_inc(product, 1)
            pe.wait_ge(merged, 2)

            def score(b, a, t):
                if not live(b, 0):
                    return
                i, tile = t // 4, t % 4
                if i % 8 == 0 and tile == 0:
                    pe.wait_ge(qk_landed[a][i // 8], cnt(b, 0, QK_ALL, QK_ALL))
                last = t - 2 if t >= 3 else (0, -2, -1)[t]
                need(pe, max_taken, cnt(b, 0, 2 * UNIT, UNIT * a + last))
                pe.matmul(score_ps[:, t % 3, :], qt[a][0:ROWS, 4 * (i // 8) + i % 4, 128 * tile:128 * tile + 128],
                          kt[a][0:ROWS, i, :], start=True, stop=True).then_inc(scored, 1)

            def shift(b, lag, a, t):
                if not live(b, lag):
                    return
                i, tile = t // 4, t % 4
                if i % 8 == 0 and tile == 0:
                    pe.wait_ge(max_landed[a], cnt(b, lag, 32, 16 * (i // 8 + 1)))
                need(pe, weighed, cnt(b, lag, 2 * UNIT, UNIT * a + t - 1))
                pe.matmul(shift_ps[:, t % 2, :], kt[a][:, i, 128 * tile:128 * tile + 128],
                          qt[a][:, 4 * (i // 8) + i % 4, :], start=True, stop=True).then_inc(shifted, 1)

            def value(b, lag, a, quad, tile):
                if not live(b, lag):
                    return
                if tile == 0:
                    if a == PLAIN:
                        pe.wait_ge(clip_dve, cnt(b, lag, 24, 6 * quad + 6))
                        pe.wait_ge(clip_pool, cnt(b, lag, 4, quad + 1))
                    else:
                        pe.wait_ge(weighed, cnt(b, lag, 2 * UNIT, UNIT + 16 * (quad + 1)))
                    if quad == 0:
                        pe.wait_ge(v_placed[a], cnt(b, lag, 2, 4))
                    if quad % 2 == 0:
                        need(pe, o_copied, cnt(b, lag, 4, 2 * a + quad // 2))
                ab = quad % 2
                for j in range(4):
                    mm = pe.matmul(o_ps[32 * j:32 * j + 32, :],
                                   vt[a][:, tile, 4 * (quad // 2) + j, 16 * ab:16 * ab + 32],
                                   weights[:, 4 * (quad % 2) + j, tile, :],
                                   start=(ab == 0 and tile == 0), stop=(ab == 1 and tile == 3))
                mm.then_inc(valued, 1)

            def side(b, job, part):
                lag = LAG[job]
                if not live(b, lag):
                    return
                to, at = bank(job), side_bank(job)
                if part == 0:
                    need(pe, side_free[at], side_uses(b, job))

                def turn(src, n=128):
                    for tile in range(NT):
                        mm = pe.transpose(to[0:n, 128 * tile:128 * tile + 128], src(tile), ident)
                    mm.then_inc(side_full[at], 1)

                if job[:4] == "max_":
                    a, gh = int(job[4:-1] == "rope"), int(job[-1])
                    pe.wait_ge(max_split, cnt(b, lag, 4, 2 * a + gh + 1))
                    for tile in range(NT):
                        mm = pe.transpose(to.bitcast(BF16)[0:24, 128 * tile:128 * tile + 128],
                                          max_parts[:, gh, tile, :], ident_bf[:, :])
                    mm.then_inc(side_full[at], 1)
                elif job[:2] == "o_":
                    a, gh = int(job[2:-1] == "rope"), int(job[-1])
                    pe.wait_ge(o_copied, cnt(b, lag, 4, 2 * a + gh + 1))
                    turn(lambda tile: o_sb[:, 128 * tile:128 * tile + 128])
                elif job[:4] == "back":
                    a = int(job == "back_rope")
                    taken(pe, b, ("o_plain1", "o_rope1")[a])
                    turn(lambda tile: heads[a][:, tile, :])
                elif job[:2] == "y_":
                    a = int(job == "y_rope")
                    taken(pe, b, ("back_plain", "back_rope")[a])
                    for tile in range(NT):
                        mm = pe.matmul(to[:, 128 * tile:128 * tile + 128], headsT[:, 128 * tile:128 * tile + 128],
                                       wo_sb[:, a, :], start=True, stop=True)
                    mm.then_inc(side_full[at], 1)
                elif job == "xnT":
                    pe.wait_ge(xn_done, cnt(b, lag, NT, NT))
                    turn(lambda tile: xn_new[:, tile, :])
                elif job in ("q_plain", "k_plain", "q_rope", "qs_rope", "k_rope", "ks_rope"):
                    taken(pe, b, "xnT")
                    w = {"q_plain": wq_sb[:, 0, :], "k_plain": wq_sb[:, 1, :], "q_rope": wq_sb[:, 2, :],
                         "qs_rope": wq_sb[:, 3, :], "k_rope": wkr_sb[:, 0, :], "ks_rope": wkr_sb[:, 1, :]}[job]
                    pe.matmul(to, w, xnT[:, :], start=True, stop=True).then_inc(side_full[at], 1)
                elif job in ("v0", "v1"):
                    for j in range(2):
                        tile = 2 * int(job[1]) + j
                        mm = pe.matmul(to[:, 256 * j:256 * j + 256], xnT[:, 128 * tile:128 * tile + 128],
                                       wv_sb[:, :, :].rearrange("p a c -> p (a c)"), start=True, stop=True)
                    mm.then_inc(side_full[at], 1)
                elif job == "x1T":
                    pe.wait_ge(x1_done, cnt(b, lag, NT, NT))
                    turn(lambda tile: x1[:, tile, :])
                elif job == "gates":
                    taken(pe, b, "x1T")
                    for tile in range(NT):
                        mm = pe.matmul(to[:, NL * tile:NL * tile + NL], x1T[:, 128 * tile:128 * tile + 128],
                                       w_gate_sb[:, :], start=True, stop=True)
                    mm.then_inc(side_full[at], 1)
                elif job[:2] == "up" or job[:4] == "down":
                    w = 2 * int(job[-1]) + int(job[0] == "d")
                    pe.matmul(to, w_up_sb[:, w, :], x1T[:, :], start=True, stop=True).then_inc(side_full[at], 1)
                elif job == "shared_out":
                    taken(pe, b + (-1), "down3")
                    for tile in (2 * part, 2 * part + 1):
                        for c in range(2):
                            mm = pe.matmul(to[:, 128 * tile:128 * tile + 128],
                                           hidden[:, c, 128 * tile:128 * tile + 128], w_out_sb[:, c, :],
                                           start=(c == 0), stop=(c == 1))
                    if part == 1:
                        mm.then_inc(side_full[at], 1)
                else:
                    n = int(job[3:])
                    tile, e = n // 2, n % 2
                    mm = pe.matmul(to, hidden[:, 2 + part, 128 * tile:128 * tile + 128],
                                   w2_sb[:, part, 512 * e:512 * e + 512], start=(part == 0), stop=(part == 1))
                    if part == 1:
                        mm.then_inc(side_full[at], 1)

            def step(b, which):
                for t in range(UNIT):
                    i = t // 4
                    unit, k = divmod(i + 11, 16)
                    if which == "even":
                        score(b, PLAIN, t)
                        shift(b, -1, ROPE, t)
                        if t % 4 == VALUE_AT:
                            value(b, -1, (PLAIN, ROPE)[unit], k // 4, k % 4)
                    else:
                        score(b, ROPE, t)
                        shift(b, 0, PLAIN, t)
                        if t % 4 == VALUE_AT:
                            value(b, unit - 1, (ROPE, PLAIN)[unit], k // 4, k % 4)
                    for job, part in jobs_at(which, t):
                        side(b, job, part)

            all_steps(pe, lambda b: step(b, "even"), lambda b: step(b, "odd"))

        @block.scalar
        def _(act):
            def weigh(b, lag, a, t):
                if not live(b, lag):
                    return
                i, tile = t // 4, t % 4
                if i % 4 == 0:
                    need(act, valued, cnt(b, lag, 32, 16 * a + 4 * (i // 4) - 7 + tile))
                act.wait_ge(shifted, cnt(b, lag, 2 * UNIT, UNIT * a + t + 1))
                act.activation(weights[:, i % 8, tile, :], shift_ps[:, t % 2, :], ACT.Exp,
                               scale=SCALE).then_inc(weighed, 1)

            def copy_max(b, job):
                lag, a, gh = LAG[job], int(job[4:-1] == "rope"), int(job[-1])
                if live(b, lag):
                    full(act, b, job)
                    need(act, max_landed[1 - a], cnt(b, lag + a - 1, 32, 16 * (gh + 1)))
                    act.activation(max_rows[:, gh, :], bank(job).bitcast(BF16)[0:24, 0:S],
                                   ACT.Copy).then_inc(free(job), 1)

            def copy_o(b, job, before, lag_before):
                lag, a, gh = LAG[job], int(job[2:-1] == "rope"), int(job[-1])
                if live(b, lag):
                    act.wait_ge(valued, cnt(b, lag, 32, 16 * a + 8 * (gh + 1)))
                    if live(b, lag_before + LAG[before]):
                        full(act, b + lag_before, before)
                    act.activation(o_sb[:, :], o_ps[:, :], ACT.Copy).then_inc(o_copied, 1)

            def copy_side(b, job, dst):
                if live(b, LAG[job]):
                    full(act, b, job)
                    act.activation(dst, bank(job), ACT.Copy).then_inc(free(job), 1)

            def weight_experts(b, n):
                if live(b, -2):
                    full(act, b, f"exp{n}")
                    act.wait_ge(route, cnt(b, -2, ROUTE_A + ROUTE_B, ROUTE_A + ROUTE_B))
                    if n >= 2:
                        act.wait_ge(mixed, cnt(b, -2, 24, 3 * (n - 2) + 1))
                    for e in range(4):
                        last = act.activation(spread[:, n % 2, e, :], bank(f"exp{n}")[:, 128 * e:128 * e + 128],
                                              ACT.Copy, scale=gate[:, n // 2, 4 * (n % 2) + e:4 * (n % 2) + e + 1])
                    last.then_inc(free(f"exp{n}"), 1)

            def even(b):
                for t in range(UNIT):
                    weigh(b, -1, ROPE, t)
                    for n in range(8):
                        if t == after("even", f"exp{n}"):
                            weight_experts(b, n)
                    if t == after("even", "max_rope1"):
                        copy_max(b, "max_rope1")
                    if t == 18:
                        copy_o(b, "o_plain1", "o_plain0", -1)
                    if t == after("even", "back_plain"):
                        copy_side(b, "back_plain", headsT[:, :])
                    if t == after("even", "max_plain0"):
                        copy_max(b, "max_plain0")
                    if t == 50:
                        copy_o(b, "o_rope0", "o_plain1", 0)

            def odd(b):
                def part(t, job, quarter, a, src, parts, hi):
                    if t == quarter and live(b, 1):
                        if hi and a == PLAIN:
                            full(act, b, job)
                        elif hi:
                            act.wait_ge(rope_done, cnt(b, 1, 2, 1 + int(job[0] == "k")))
                        if hi:
                            for gh in range(2):
                                need(act, qk_landed[a][gh], cnt(b, 1, QK_ALL, 0))
                            act.activation(parts[a][:, 0, :], src, ACT.Copy).then_inc(hi_done[a], 1)
                        else:
                            if a == PLAIN:
                                taken(act, b, job)
                            else:
                                act.wait_ge(rope_rest, cnt(b, 1, 2, 1 + int(job[0] == "k")))
                            act.activation(parts[a][:, 1, :], src, ACT.Copy).then_inc(mid_done[a], 1)

                for t in range(UNIT):
                    weigh(b, 0, PLAIN, t)
                    if t == after("odd", "max_plain1"):
                        copy_max(b, "max_plain1")
                    if t == after("odd", "xnT"):
                        copy_side(b, "xnT", xnT[:, :])
                    part(t, "q_plain", after("odd", "q_plain"), PLAIN, bank("q_plain"), q_parts, True)
                    part(t, "q_plain", after("odd", "q_plain", 3), PLAIN, q_rest[:, :], q_parts, False)
                    part(t, "k_plain", after("odd", "k_plain"), PLAIN, bank("k_plain"), k_parts, True)
                    part(t, "k_plain", after("odd", "k_plain", 3), PLAIN, k_rest[:, :], k_parts, False)
                    if t == 18:
                        copy_o(b, "o_rope1", "o_rope0", 0)
                    if t == after("odd", "back_rope"):
                        copy_side(b, "back_rope", headsT[:, :])
                    part(t, "q_rope", 35, ROPE, roped[:, 0, :], q_parts, True)
                    if t == after("odd", "x1T"):
                        copy_side(b, "x1T", x1T[:, :])
                    if t == after("odd", "max_rope0"):
                        copy_max(b, "max_rope0")
                    part(t, "k_rope", 40, ROPE, roped[:, 1, :], k_parts, True)
                    for n in range(4):
                        if t == after("odd", f"up{n}") and live(b, -1):
                            full(act, b, f"up{n}")
                            if n:
                                taken(act, b, f"up{n - 1}")
                            act.activation(tanh[:, :], bank(f"up{n}"), ACT.Tanh, scale=0.5).then_inc(tanh_done, 1)
                    part(t, "q_rope", 44, ROPE, q_rest[:, :], q_parts, False)
                    part(t, "k_rope", 46, ROPE, k_rest[:, :], k_parts, False)
                    if t == 55 and live(b, -1):
                        act.wait_ge(route, cnt(b, -1, ROUTE_A + ROUTE_B, ROUTE_A))
                        act.activation(ez[:], z[:], ACT.Exp).then_inc(z_exp, 1)
                    if t == 50:
                        copy_o(b, "o_plain0", "o_rope1", 0)
                    for n in range(2):
                        if t == after("odd", f"v{n}", 1) and live(b, 1):
                            for a in range(2):
                                need(act, v_placed[a], cnt(b, 1, 2, 2))
                            copy_side(b, f"v{n}", v_stage[:, 2 * n:2 * n + 2, :, :].rearrange("p t a c -> p (t a c)"))

            all_steps(act, even, odd)

        @block.vector
        def _(dve):
            for a in range(2):
                dve.memset(kt[a][:, :, :].bitcast(F32), 0.0).then_inc(kt_made, 1)
            dve.wait_ge(kt_made, 2)
            for a in range(2):
                own = kt[a][:, :, :].rearrange("p (g ab c) n -> p g ab c n", g=2, ab=2)
                for gh in range(2):
                    dve.memset(own[ROWS:ROWS + 3, gh, 0], 1.0).then_inc(kt_made, 1)
                    dve.memset(own[ROWS:ROWS + 6, gh, 1], 1.0).then_inc(kt_made, 1)
            dve.wait_ge(kt_made, 2 + 8)
            for a in range(2):
                own = kt[a][:, :, :].rearrange("p (g ab c) n -> p g ab c n", g=2, ab=2)
                for gh in range(2):
                    dve.memset(own[ROWS:ROWS + 3, gh, 1], 0.0).then_inc(kt_made, 1)
            dve.wait_ge(loaded, 16 * len(LOADS))
            dve.tensor_copy(ident_bf[:, :], ident).then_inc(kt_made, 1)
            dve.wait_ge(product, 1)
            dve.tensor_copy(wkr_sb[:, :, :].rearrange("p a c -> p (a c)"), side_ps[:, 0, 0:256]).then_inc(merged, 1)
            dve.tensor_copy(wv_sb[:, 1, :], side_ps[:, 0, 256:384]).then_inc(merged, 1)

            def maximum(b, a, t):
                if not live(b, 0):
                    return
                i, tile = t // 4, t % 4
                if t % 32 == 0:
                    need(dve, max_split, cnt(b, 0, 4, 2 * a + i // 8 - 1))
                dve.wait_ge(scored, cnt(b, 0, 2 * UNIT, UNIT * a + t + 1))
                dve.tensor_reduce(negmax[:, i // 8, tile, i % 8:i % 8 + 1], score_ps[:, t % 3, :], AX.X, ALU.max,
                                  negate=True).then_inc(max_taken, 1)

            def clip(b, lag, i, part):
                if live(b, lag):
                    dve.wait_ge(weighed, cnt(b, lag, 2 * UNIT, NT * i + 2 * part + 2))
                    half = weights[:, i % 8, 2 * part:2 * part + 2]
                    dve.tensor_scalar(half, half, FLOOR, None, ALU.max).then_inc(clip_dve, 1)

            def normalise(b, job):
                lag, a, gh = LAG[job], int(job[2:-1] == "rope"), int(job[-1])
                if not live(b, lag):
                    return
                full(dve, b, job)
                o = bank(job).rearrange("p (t h c) -> p t h c", t=NT, h=8)
                dve.tensor_scalar(den[:], o[:, :, :, DH], EPS_DEN if a == PLAIN else 0.0, None,
                                  ALU.add).then_inc(den_done, 1)
                dve.wait_ge(den_done, cnt(b, lag, 4, 2 * a + gh + 1))
                dve.reciprocal(inv_den[:], den[:]).then_inc(inv_done, 1)
                dve.wait_ge(inv_done, cnt(b, lag, 4, 2 * a + gh + 1))
                dve.tensor_tensor(heads[a][:, :, 64 * gh:64 * gh + 64].rearrange("p t (h c) -> p t h c", h=8),
                                  o[:, :, :, 0:DH], inv_den[:].unsqueeze(3).broadcast_to([128, NT, 8, DH]),
                                  ALU.mult).then_inc(free(job), 1)

            def add_side(b, job, dst, other):
                full(dve, b, job)
                dve.tensor_tensor(dst, tiles(bank(job)), other, ALU.add).then_inc(free(job), 1)

            def even(b):
                for t in range(UNIT):
                    maximum(b, PLAIN, t)
                    if t in (1, 2):
                        clip(b, -1, H - 1, t - 1)
                    if t == after("even", "shared_out") and live(b, -2):
                        add_side(b, "shared_out", x1[:], x1[:])
                    if t == after("even", "o_plain1"):
                        normalise(b, "o_plain1")
                    if t == after("even", "y_plain") and live(b, -1):
                        dve.wait_ge(res_landed, cnt(b, -1, 16, 16))
                        add_side(b, "y_plain", res_new[:], res_new[:])
                    if t == after("even", "o_rope0"):
                        normalise(b, "o_rope0")
                    if t == 44 and live(b, 1):
                        dve.wait_ge(x_landed, cnt(b, 1, 16, 16))
                        need(dve, rstd_done, cnt(b, 1, 1, 0))
                        for tile in range(NT):
                            dve.bn_stats(stats[:, tile, :], x_in[:, tile, :]).then_inc(stats_done, 1)
                    if t == 46 and live(b, 1):
                        dve.wait_ge(stats_done, cnt(b, 1, NT, NT))
                        stand(dve)
                        for tile in range(NT):
                            dve.bn_aggr(moments[:, tile, :], stats[:, tile, :]).then_inc(moments_done, 1)
                    if t == 61 and live(b, 1):
                        dve.wait_ge(rstd_done, cnt(b, 1, 1, 1))
                        need(dve, mid_landed, cnt(b, 1, 16, 0))
                        for tile in range(NT):
                            dve.tensor_scalar(xn_new[:, tile, :], x_in[:, tile, :], moments[:, tile, 0:1],
                                              ln_rstd[:, tile:tile + 1], ALU.subtract, ALU.mult).then_inc(xn_done, 1)

            def odd(b):
                def scale(dst, which, lag, signal):
                    dve.wait_ge(rms_done, norms_done(b, lag, which) + 1)
                    for tile in range(NT):
                        dve.scalar_tensor_tensor(out=dst[:, tile, :], in0=x1[:, tile, :],
                                                 scalar=rms[:, which, tile:tile + 1], in1=norm_sb[:, which, :],
                                                 op0=ALU.mult, op1=ALU.mult).then_inc(signal, 1)

                def mean_square(which, lag):
                    dve.wait_ge(squared, norms_done(b, lag, which) + 1)
                    dve.tensor_reduce(sums[:, which, :], square, AX.X, ALU.add).then_inc(summed, 1)

                for t in range(UNIT):
                    maximum(b, ROPE, t)
                    if t % 4 in (1, 2) and t > 4 and (t // 4 - 1) % 4:
                        clip(b, 0, t // 4 - 1, t % 4 - 1)
                    if t == 3 and live(b, -2):
                        mean_square(1, -2)
                    if t == 8 and live(b, -2):
                        need(dve, stored, cnt(b, -2, 16, 0))
                        scale(out_sb, 1, -2, scaled)
                    for job, rest, quarter in (("q_plain", q_rest, 6), ("k_plain", k_rest, 12)):
                        if t == quarter and live(b, 1):
                            dve.wait_ge(hi_done[PLAIN], cnt(b, 1, 2, 1 + int(job[0] == "k")))
                            need(dve, mid_done[ROPE], cnt(b, 1, 2, 0))
                            need(dve, lo_done[ROPE], cnt(b, 1, 2, 0))
                            parts = q_parts if job[0] == "q" else k_parts
                            dve.tensor_tensor(rest[:, :], bank(job), parts[PLAIN][:, 0, :],
                                              ALU.subtract).then_inc(free(job), 1)
                    if t == after("odd", "o_rope1"):
                        normalise(b, "o_rope1")
                    if t == after("odd", "y_rope") and live(b, -1):
                        dve.wait_ge(old_landed, cnt(b, -1, 16, 16))
                        need(dve, scaled, cnt(b, -2, NT, NT))
                        add_side(b, "y_rope", x1[:], xn_old[:])
                    if t == 29 and live(b, -1):
                        mean_square(0, -1)
                    if t == 34 and live(b, -1):
                        scale(x1, 0, -1, x1_done)
                    for job, dst, table in (("q_rope", roped[:, 0, :], cos), ("qs_rope", turned[:, :], sin),
                                            ("k_rope", roped[:, 1, :], cos), ("ks_rope", turned[:, :], sin)):
                        if t == after("odd", job) and live(b, 1):
                            full(dve, b, job)
                            need(dve, rope_rest, cnt(b, 1, 2, 0))
                            if job == "ks_rope":
                                dve.wait_ge(rope_done, cnt(b, 1, 2, 1))
                            dve.tensor_tensor(dst, bank(job), table, ALU.mult).then_inc(free(job), 1)
                    if t == after("odd", "gates") and live(b, -1):
                        full(dve, b, "gates")
                        dve.tensor_tensor(logits[:], bank("gates")[:, 0:NT * NL].rearrange("p (t l) -> p t l", t=NT),
                                          bias_sb[:, :].unsqueeze(1).broadcast_to([128, NT, NL]),
                                          ALU.add).then_inc(free("gates"), 1)
                    if t == 53 and live(b, -1):
                        dve.wait_ge(route, cnt(b, -1, ROUTE_A + ROUTE_B, ROUTE_A - 1))
                        dve.tensor_reduce(top[:], sel0[:], AX.X, ALU.max).then_inc(top_done, 1)
                    if t == 57 and live(b, -1):
                        dve.wait_ge(z_exp, cnt(b, -1, 1, 1))
                        dve.tensor_scalar(total[:, :, 0:1], ez[:, :, 0:1], 1.0, None, ALU.add).then_inc(shares_done, 1)
                        dve.tensor_reduce(total[:, :, 1:2], ez[:, :, 1:], AX.X, ALU.add).then_inc(shares_done, 1)
                        dve.wait_ge(shares_done, cnt(b, -1, 3, 2))
                        dve.reciprocal(share[:], total[:]).then_inc(shares_done, 1)
                    for n in range(4):
                        if t == after("odd", f"up{n}", 2) and live(b, -1):
                            dve.wait_ge(tanh_done, cnt(b, -1, 4, n + 1))
                            dve.scalar_tensor_tensor(out=hidden[:, n, :], in0=tanh[:, :], scalar=1.0,
                                                     in1=bank(f"up{n}"), op0=ALU.add,
                                                     op1=ALU.mult).then_inc(free(f"up{n}"), 1)
                        if t == after("odd", f"down{n}", 1) and live(b, -1):
                            full(dve, b, f"down{n}")
                            taken(dve, b, f"up{n}")
                            dve.scalar_tensor_tensor(out=hidden[:, n, :], in0=hidden[:, n, :], scalar=0.5,
                                                     in1=bank(f"down{n}"), op0=ALU.mult,
                                                     op1=ALU.mult).then_inc(free(f"down{n}"), 1)
                    if t == after("odd", "o_plain0"):
                        normalise(b, "o_plain0")

            all_steps(dve, even, odd)

        @block.gpsimd
        def _(pool):
            pool.memset(minus_half[:, :], -0.5).then_inc(ready, 1)
            for e in range(EPG):
                pool.memset(rank0[:, :, e:e + 1], float(EPG - 1 - e)).then_inc(ready, 1)
            for a in range(2):
                pool.memset(vt[a][:], 0.0).then_inc(ready, 1)
            pool.wait_ge(ready, READY)
            for a in range(2):
                for ab in range(2):
                    pool.memset(vt[a][:, :, :, 32 * ab + DH:32 * ab + DH + 1], 1.0).then_inc(v_placed[a], 1)

            def split_max(b, job):
                lag, a, gh = LAG[job], int(job[4:-1] == "rope"), int(job[-1])
                if not live(b, lag):
                    return
                n = cnt(b, lag, 4, 2 * a + gh + 1)

                def part(k):
                    return max_parts[:, gh].rearrange("p t (ab k g) -> p t ab k g", ab=2, k=3)[:, :, :, k, :]

                def heads_of(ap):
                    return ap.rearrange("p t (ab g) -> p t ab g", ab=2)

                pool.wait_ge(max_taken, cnt(b, lag, 2 * UNIT, UNIT * a + 32 * (gh + 1)))
                stand(pool)
                pool.tensor_copy(part(0), heads_of(negmax[:, gh])).then_inc(max_hi, 1)
                pool.wait_ge(max_hi, n)
                pool.tensor_tensor(heads_of(max_rest[:]), heads_of(negmax[:, gh]), part(0), ALU.subtract)\
                    .then_inc(max_r, 1)
                pool.wait_ge(max_r, n)
                stand(pool)
                pool.tensor_copy(part(1), heads_of(max_rest[:])).then_inc(max_mid, 1)
                pool.wait_ge(max_mid, n)
                pool.tensor_tensor(part(2), heads_of(max_rest[:]), part(1), ALU.subtract).then_inc(max_split, 1)

            def place_v(b, a):
                if not live(b, 0):
                    return
                taken(pool, b + (-1), "v1")
                need(pool, valued, cnt(b, -1, 32, 16 * (a + 1)))
                stand(pool)
                for ab in range(2):
                    src = v_stage[:, :, a, :].rearrange("p t (h ab c) -> p t h ab c", ab=2, c=DH)[:, :, :, ab, :]
                    pool.tensor_copy(vt[a][:, :, :, 32 * ab:32 * ab + DH], src).then_inc(v_placed[a], 1)

            def root(b, lag, which):
                pool.wait_ge(summed, norms_done(b, lag, which) + 1)
                stand(pool)
                pool.tensor_scalar(sums[:, which, :], sums[:, which, :], 1.0 / D, EPS_RMS, ALU.mult,
                                   ALU.add).then_inc(mean_done, 1)
                pool.wait_ge(mean_done, norms_done(b, lag, which) + 1)
                pool.tensor_tensor(rms[:, which, :], sums[:, which, :], minus_half[:, :], ALU.pow).then_inc(rms_done, 1)

            def clip(b, i):
                if live(b, 0):
                    pool.wait_ge(weighed, cnt(b, 0, 2 * UNIT, NT * (i + 1)))
                    stand(pool)
                    pool.tensor_scalar(weights[:, i % 8], weights[:, i % 8], FLOOR, None, ALU.max).then_inc(clip_pool, 1)

            def router(b, first):
                k = [0 if first else ROUTE_A]
                base = lambda n: cnt(b, -1, ROUTE_A + ROUTE_B, n)

                def then(ins):
                    k[0] += 1
                    ins.then_inc(route, 1)
                    pool.wait_ge(route, base(k[0]))
                    stand(pool)

                def wide(ap, n):
                    return ap.broadcast_to([128, NT, n])

                tt = pool.tensor_tensor
                in0, in1 = in_group[:, 0], in_group[:, 1]
                le = logits[:, :, G:NL]
                if first:
                    taken(pool, b, "gates")
                    taken(pool, b, "exp7")
                    then(tt(gap[:], logits[:, :, 0:1], logits[:, :, 1:2], ALU.subtract))
                    then(pool.tensor_scalar(in0, gap[:], 0.0, None, ALU.is_ge))
                    then(pool.tensor_scalar(in1, in0, -1.0, 1.0, ALU.mult, ALU.add))
                    then(pool.tensor_scalar(low[:], gap[:], 0.0, 2.0, ALU.min, ALU.mult))
                    then(tt(z[:, :, 0:1], low[:], gap[:], ALU.subtract))
                    then(tt(sel0[:], le[:, :, 0:EPG], wide(in0, EPG), ALU.mult))
                    then(tt(sel1[:], le[:, :, EPG:E], wide(in1, EPG), ALU.mult))
                    then(tt(sel0[:], sel0[:], sel1[:], ALU.add))
                    pool.wait_ge(top_done, cnt(b, -1, 1, 1))
                    then(tt(z[:, :, 1:], sel0[:], wide(top[:], EPG), ALU.subtract))
                    assert k[0] == ROUTE_A
                    return
                pool.wait_ge(shares_done, cnt(b, -1, 3, 3))
                then(tt(prob[:], ez[:, :, 1:], wide(share[:, :, 1:2], EPG), ALU.mult))
                then(tt(prob[:], prob[:], wide(share[:, :, 0:1], EPG), ALU.mult))
                for s in range(1, EPG):
                    c, n = above[s - 1], EPG - s
                    then(tt(c[:], prob[:, :, 0:n], prob[:, :, s:EPG], ALU.subtract))
                    then(pool.tensor_scalar(c[:], c[:], 0.0, None, ALU.is_ge))
                    then(tt(rank[:, :, s:EPG], (rank0 if s == 1 else rank)[:, :, s:EPG], c[:], ALU.add))
                    if s == 1:
                        then(tt(rank[:, :, 0:1], rank0[:, :, 0:1], c[:, :, 0:1], ALU.subtract))
                        then(tt(rank[:, :, 1:n], rank[:, :, 1:n], c[:, :, 1:n], ALU.subtract))
                    else:
                        then(tt(rank[:, :, 0:n], rank[:, :, 0:n], c[:], ALU.subtract))
                then(pool.tensor_scalar(rank[:], rank[:], 1.5, None, ALU.is_lt))
                then(tt(prob[:], prob[:], rank[:], ALU.mult))
                then(tt(gate[:, :, 0:EPG], prob[:], wide(in0, EPG), ALU.mult))
                then(tt(gate[:, :, EPG:E], prob[:], wide(in1, EPG), ALU.mult))
                assert k[0] == ROUTE_A + ROUTE_B

            def mix(b, n):
                if live(b, -2):
                    taken(pool, b, f"exp{n}")
                    taken(pool, b, "shared_out")
                    pool.tensor_tensor(two[:], spread[:, n % 2, 0:2, :], spread[:, n % 2, 2:4, :],
                                       ALU.add).then_inc(mixed, 1)
                    pool.wait_ge(mixed, cnt(b, -2, 24, 3 * n + 1))
                    pool.tensor_tensor(one[:, :], two[:, 0, :], two[:, 1, :], ALU.add).then_inc(mixed, 1)
                    pool.wait_ge(mixed, cnt(b, -2, 24, 3 * n + 2))
                    pool.tensor_tensor(x1[:, n // 2, :], x1[:, n // 2, :], one[:, :], ALU.add).then_inc(mixed, 1)
                    pool.wait_ge(mixed, cnt(b, -2, 24, 3 * n + 3))

            def even(b):
                split_max(b, "max_rope1")
                mix(b, 0)
                place_v(b, PLAIN)
                mix(b, 1)
                mix(b, 2)
                mix(b, 3)
                split_max(b, "max_plain0")
                mix(b, 4)
                mix(b, 5)
                if live(b, 1):
                    pool.wait_ge(moments_done, cnt(b, 1, NT, NT))
                    stand(pool)
                    pool.tensor_scalar(ln_var[:, :], moments[:, :, 1], EPS_LN, None, ALU.add).then_inc(var_done, 1)
                    pool.wait_ge(var_done, cnt(b, 1, 1, 1))
                    need(pool, xn_done, cnt(b, 1, NT, 0))
                    pool.tensor_tensor(ln_rstd[:, :], ln_var[:, :], minus_half[:, :], ALU.pow).then_inc(rstd_done, 1)
                mix(b, 6)
                mix(b, 7)

            def odd(b):
                split_max(b, "max_plain1")
                if live(b, -2):
                    pool.tensor_tensor(square, x1[:], x1[:], ALU.mult).then_inc(squared, 1)
                    root(b, -2, 1)
                clip(b, 0)
                if live(b, -2):
                    pool.wait_ge(scaled, cnt(b, -2, NT, NT))
                    pool.wait_ge(res_moved, cnt(b, -2, 16, 16))
                    pool.tensor_tensor(out_sb[:], out_sb[:], res_old[:], ALU.add).then_inc(final_done, 1)
                if live(b, 1):
                    for n, (job, rest, parts) in enumerate((("q_plain", q_rest, q_parts), ("k_plain", k_rest, k_parts))):
                        pool.wait_ge(mid_done[PLAIN], cnt(b, 1, 2, n + 1))
                        pool.tensor_tensor(parts[PLAIN][:, 2, :], rest[:, :], parts[PLAIN][:, 1, :],
                                           ALU.subtract).then_inc(lo_done[PLAIN], 1)
                place_v(b, ROPE)
                clip(b, 4)
                if live(b, -1):
                    taken(pool, b, "y_rope")
                    pool.tensor_tensor(square, x1[:], x1[:], ALU.mult).then_inc(squared, 1)
                    root(b, -1, 0)

                def turn(n, last):
                    if live(b, 1):
                        taken(pool, b, ("q_rope", "k_rope")[n])
                        taken(pool, b, last)
                        pool.tensor_tensor(roped[:, n, :], roped[:, n, :], turned[:, :], ALU.add).then_inc(rope_done, 1)

                turn(0, "qs_rope")
                split_max(b, "max_rope0")
                turn(1, "ks_rope")
                if live(b, 1):
                    for n, (rest, parts) in enumerate(((q_rest, q_parts), (k_rest, k_parts))):
                        pool.wait_ge(hi_done[ROPE], cnt(b, 1, 2, n + 1))
                        pool.wait_ge(mid_done[PLAIN], cnt(b, 1, 2, 2))
                        pool.tensor_tensor(rest[:, :], roped[:, n, :], parts[ROPE][:, 0, :],
                                           ALU.subtract).then_inc(rope_rest, 1)
                clip(b, 8)
                if live(b, -1):
                    router(b, True)
                clip(b, 12)
                if live(b, 1):
                    for n, (rest, parts) in enumerate(((q_rest, q_parts), (k_rest, k_parts))):
                        pool.wait_ge(mid_done[ROPE], cnt(b, 1, 2, n + 1))
                        pool.tensor_tensor(parts[ROPE][:, 2, :], rest[:, :], parts[ROPE][:, 1, :],
                                           ALU.subtract).then_inc(lo_done[ROPE], 1)
                if live(b, -1):
                    router(b, False)

            all_steps(pool, even, odd)


def kernel(**inputs):
    import concourse.bacc as _bacc
    from concourse.bass_utils import run_bass_kernel_spmd as _run

    g = {k.replace("L0_", ""): np.asarray(v) for k, v in inputs.items()}

    def in_order(w):
        return w.reshape(-1, 2, 4, 2, DH).transpose(0, 1, 3, 4, 2).reshape(-1, 128)

    def swapped(w):
        return w.reshape(-1, 64, 2)[:, :, ::-1].reshape(-1, 128)

    wqkv = g["attn_Wqkv"].T
    wq, wk = g["ffn_Wq"], g["ffn_Wk"]
    up = np.stack([g["ffn_W_shared_in"], g["ffn_W1_shared"]], 1).reshape(D, 2, 2, 2, 128)
    inv = (1.0 / 10000.0 ** (np.arange(0, DH, 2, dtype=np.float32) / DH)).astype(np.float32)
    ang = np.arange(S, dtype=np.float32)[:, None] * inv[None, :]
    sign = np.array([-1.0, 1.0] * (DH // 2), np.float32)
    by_d = [np.repeat(np.cos(ang), 2, 1).T, np.repeat(np.sin(ang), 2, 1).T * sign[:, None]]
    rows = [np.broadcast_to(t[None, :, None, :], (4, DH, 4, S)).reshape(128, S) for t in by_d]
    arrays = {
        "x": g["attn_x"].reshape(B, NT, 128, D).transpose(0, 2, 1, 3),
        "wq": np.stack([in_order(wqkv[:, 0:128]), in_order(wqkv[:, 128:256]), in_order(wq), in_order(swapped(wq))], 1),
        "wkcT": g["ffn_Wk_c"].T,
        "wk": np.stack([in_order(wk), in_order(swapped(wk))], 1),
        "wvcT": g["ffn_Wv_c"].T,
        "wvp": wqkv[:, 256:384],
        "wvr": g["ffn_Wv"],
        "wo": np.stack([g["attn_Wout"].T, g["ffn_Wo"]], 1),
        "w_up": up.transpose(0, 1, 3, 2, 4).reshape(D, 8, 128),
        "w_out": g["ffn_W_shared_out"].reshape(2, 128, D).transpose(1, 0, 2),
        "w2": g["ffn_W2_experts"].reshape(E, 2, 128, D).transpose(2, 1, 0, 3).reshape(128, 2, E * D),
        "w_gate": np.concatenate([g["ffn_Wg_gate"], g["ffn_We_gate"]], 1),
        "bias": np.concatenate([g["ffn_group_bias"], g["ffn_expert_bias"]])[None],
        "norms": np.stack([g["ffn_norm1_w"], g["ffn_norm2_w"]])[None],
        "consts": np.concatenate([np.eye(128, dtype=np.float32)] + rows, 1),
    }
    nc = _bacc.Bacc("TRN2", target_bir_lowering=False, num_devices=1, dynamic_dma_scratch_size=1024)
    feeds, aps = {}, {}
    for name, a in arrays.items():
        a = np.ascontiguousarray(a)
        feeds[f"in_{name}_dram"] = a
        aps[name] = nc.dram_tensor(f"in_{name}_dram", a.shape, mybir.dt.from_np(a.dtype), kind="ExternalInput").ap()
    out = nc.dram_tensor("out_0_dram", (B, 128, NT, D), F32, kind="ExternalOutput").ap()
    nc.disable_value_cache = True
    layer_kernel(nc, out=out, **aps)
    r = _run(nc, [feeds], core_ids=[0])
    y = r.results[0]["out_0_dram"]
    return y.reshape(B, 128, NT, D).transpose(0, 2, 1, 3).reshape(B, S, D)
```

```python
from contextlib import ExitStack

import numpy as np

import concourse.bass as bass
from concourse import mybir

ALU = mybir.AluOpType
ACT = mybir.ActivationFunctionType
AX = mybir.AxisListType
F32 = mybir.dt.float32
BF16 = mybir.dt.bfloat16

B, S, D = 16, 512, 128
H, DH = 16, 8
NT = S // 128
E, G, EPG = 8, 2, 4
NL = G + E
TERMS = 6
ROWS = TERMS * 2 * DH
MROWS = 6
Q_PART = [0, 1, 0, 1, 2, 0]
K_PART = [0, 0, 1, 1, 0, 2]
VALUE_AT = 1
UNIT = H * NT
SCALE = float(1.0 / np.sqrt(DH))
FLOOR = float(np.exp(np.float32(-50.0)))
EPS_DEN, EPS_LN, EPS_RMS = 1e-6, 1e-5, 1e-6
PLAIN, ROPE = 0, 1
QK_DMAS = TERMS * 3
VW = 48

EVEN = [("x1T", [0]), ("gates", [3]), ("max_rope1", [6]), ("q_rope", [8]), ("qs_rope", [10]), ("k_rope", [11]),
        ("ks_rope", [15]), ("up0", [16]), ("down0", [19]), ("o_plain1", [20]), ("back_plain", [23]),
        ("y_plain", [26]), ("up1", [28]), ("down1", [31]), ("up2", [35]), ("max_plain0", [36]),
        ("down2", [39]), ("up3", [43]), ("down3", [47]), ("o_rope0", [52]), ("v0", [55]), ("v1", [59])]
ODD = [("xnT", [0]), ("q_plain", [4]), ("max_plain1", [7]), ("k_plain", [10]), ("shared_out", [12, 14]),
       ("exp0", [16, 18]), ("o_rope1", [20]), ("back_rope", [23]), ("y_rope", [26]), ("exp1", [27, 28]),
       ("exp2", [29, 31]), ("exp3", [34, 36]), ("max_rope0", [38]), ("exp4", [40, 42]), ("exp5", [44, 46]),
       ("exp6", [48, 50]), ("o_plain0", [52]), ("exp7", [55, 58])]
TABLE = {"even": EVEN, "odd": ODD}
LAG = {"x1T": -2, "gates": -2, "max_rope1": -1, "q_rope": 0, "qs_rope": 0, "k_rope": 0, "ks_rope": 0,
       "o_plain1": -1, "back_plain": -1, "y_plain": -1, "max_plain0": 0, "o_rope0": -1, "v0": 0, "v1": 0,
       "xnT": 1, "q_plain": 1, "max_plain1": 0, "k_plain": 1, "shared_out": -2, "o_rope1": -1,
       "back_rope": -1, "y_rope": -1, "max_rope0": 0, "o_plain0": 0}
LAG |= {f"exp{n}": -2 for n in range(8)}
LAG |= {f"{w}{n}": -2 for n in range(4) for w in ("up", "down")}
ORDER = [name for name, _ in EVEN + ODD]
FIRST_LOOP, LAST_LOOP = 3, B - 2


def live(b, lag):
    return not isinstance(b, int) or 0 <= b + lag < B


def side_bank(job):
    return ORDER.index(job) % 2


def side_uses(b, job):
    bank, at = side_bank(job), ORDER.index(job)
    same = [n for n in ORDER if side_bank(n) == bank]
    before = [n for n in same if ORDER.index(n) < at]
    if not isinstance(b, int):
        head = sum(live(c, LAG[n]) for c in range(-1, FIRST_LOOP) for n in same)
        return (b + (-FIRST_LOOP)) * len(same) + (head + len(before))
    return sum(live(c, LAG[n]) for c in range(-1, b) for n in same) + sum(live(b, LAG[n]) for n in before)


def cnt(b, lag, per, k):
    return b * per + (lag * per + k)


def need(eng, semaphore, value):
    if not isinstance(value, int) or value > 0:
        eng.wait_ge(semaphore, value)


def after(step, job, quarters=1):
    return dict(TABLE[step])[job][-1] + quarters


def score_bank(a, t):
    return (t + a) % 3


def jobs_at(step, t):
    return [(name, at.index(t)) for name, at in TABLE[step] if t in at]


def layer_kernel(nc, x, wq, wkcT, wk, wvcT, wvp, wvr, wo, w_up, w_out, w2, w_gate, bias, norms, consts, out):
    ctx = ExitStack()
    with ctx:
        def sb(name, shape, dt=F32):
            return ctx.enter_context(nc.sbuf_tensor(name, shape, dt))

        def sem(name):
            return ctx.enter_context(nc.semaphore(name))

        score_ps = ctx.enter_context(nc.psum_tensor("score_ps", [128, 3, 512], F32))
        shift_ps = ctx.enter_context(nc.psum_tensor("shift_ps", [128, 2, 512], F32))
        o_ps = ctx.enter_context(nc.psum_tensor("o_ps", [128, 512], F32))
        side_ps = ctx.enter_context(nc.psum_tensor("side_ps", [128, 2, 512], F32))

        wq_sb = sb("wq_sb", [128, 4, 128])
        wkr_sb = sb("wkr_sb", [128, 2, 128])
        wv_sb = sb("wv_sb", [128, 2, 128])
        wo_sb = sb("wo_sb", [128, 2, 128])
        w_up_sb = sb("w_up_sb", [128, 8, 128])
        w_out_sb = sb("w_out_sb", [128, 2, 128])
        w2_sb = sb("w2_sb", [128, 2, E * 128])
        w_gate_sb = sb("w_gate_sb", [128, NL])
        bias_sb = sb("bias_sb", [128, NL])
        norm_sb = sb("norm_sb", [128, 2, 128])
        const_sb = sb("const_sb", [128, 128 + 2 * S])
        ident = const_sb[:, 0:128]
        cos = const_sb[:, 128:128 + S]
        sin = const_sb[:, 128 + S:128 + 2 * S]
        ident_bf = sb("ident_bf", [128, 128], BF16)
        minus_half = sb("minus_half", [128, NT])
        rank0 = sb("rank0", [128, NT, EPG])

        qt = [sb(f"qt{a}", [ROWS + MROWS, H // 2, S], BF16) for a in range(2)]
        kt = [sb(f"kt{a}", [ROWS + MROWS, H, S], BF16) for a in range(2)]
        vt = [sb(f"vt{a}", [128, NT, H // 2, VW]) for a in range(2)]
        v_stage = sb("v_stage", [128, NT, 2, 128])
        q_parts = [sb(f"q_parts{a}", [128, 3, S], BF16) for a in range(2)]
        k_parts = [sb(f"k_parts{a}", [128, 3, S], BF16) for a in range(2)]
        q_rest = sb("q_rest", [128, S])
        k_rest = sb("k_rest", [128, S])
        roped = sb("roped", [128, 2, S])
        turned = sb("turned", [128, S])
        weights = sb("weights", [128, 8, NT, S])
        factors = weights[0:32, 0, :, :].rearrange("p t n -> p (t n)")
        wkcT_sb, wvcT_sb, wvr_sb = (factors[:, 128 * n:128 * n + 128] for n in range(3))
        wk_sb = factors[:, 384:640].rearrange("p (a n) -> p a n", a=2)
        negmax = sb("negmax", [128, 2, NT, 8])
        max_rest = sb("max_rest", [128, NT, 8])
        max_parts = sb("max_parts", [128, 2, NT, 24], BF16)
        max_rows = sb("max_rows", [24, 2, S], BF16)
        o_sb = sb("o_sb", [128, S])
        den = sb("den", [128, NT, 8])
        inv_den = sb("inv_den", [128, NT, 8])
        heads = [sb(f"heads{a}", [128, NT, 128]) for a in range(2)]
        headsT = sb("headsT", [128, S])

        x_in = sb("x_in", [128, NT, 128])
        stats = sb("stats", [128, NT, 6])
        moments = sb("moments", [128, NT, 2])
        ln_var = sb("ln_var", [128, NT])
        ln_rstd = sb("ln_rstd", [128, NT])
        xn_new = sb("xn_new", [128, NT, 128])
        xn_mid = sb("xn_mid", [128, NT, 128])
        xn_old = sb("xn_old", [128, NT, 128])
        xnT = sb("xnT", [128, S])
        res_new = sb("res_new", [128, NT, 128])
        res_old = sb("res_old", [128, NT, 128])
        x1 = sb("x1", [128, NT, 128])
        out_sb = sb("out_sb", [128, NT, 128])
        sums = sb("sums", [128, 2, NT])
        rms = sb("rms", [128, 2, NT])
        x1T = sb("x1T", [128, S])
        tanh = sb("tanh", [128, S])
        square = tanh[:, :].rearrange("p (t c) -> p t c", t=NT)
        spread = sb("spread", [128, 2, 4, 128])
        two = sb("two", [128, 2, 128])
        one = sb("one", [128, 128])
        hidden = sb("hidden", [128, 4, S])
        logits = sb("logits", [128, NT, NL])
        in_group = sb("in_group", [128, 2, NT, 1])
        gap = sb("gap", [128, NT, 1])
        low = sb("low", [128, NT, 1])
        sel0 = sb("sel0", [128, NT, EPG])
        sel1 = sb("sel1", [128, NT, EPG])
        top = sb("top", [128, NT, 1])
        z = sb("z", [128, NT, 1 + EPG])
        ez = sb("ez", [128, NT, 1 + EPG])
        total = sb("total", [128, NT, 2])
        share = sb("share", [128, NT, 2])
        prob = sb("prob", [128, NT, EPG])
        above = [sb(f"above{s}", [128, NT, EPG - s]) for s in range(1, EPG)]
        rank = sb("rank", [128, NT, EPG])
        gate = sb("gate", [128, NT, E])

        loaded_first = sem("loaded_first")
        loaded = sem("loaded")
        kt_zeroed = sem("kt_zeroed")
        kt_ones = sem("kt_ones")
        ready = sem("ready")
        passed = sem("passed")
        product = sem("product")
        merged = sem("merged")
        x_landed = sem("x_landed")
        stats_done = sem("stats_done")
        moments_done = sem("moments_done")
        var_done = sem("var_done")
        rstd_done = sem("rstd_done")
        xn_done = sem("xn_done")
        mid_landed = sem("mid_landed")
        old_landed = sem("old_landed")
        hi_done = [sem("hi_plain"), sem("hi_rope")]
        mid_done = [sem("mid_plain"), sem("mid_rope")]
        lo_done = [sem("lo_plain"), sem("lo_rope")]
        rope_done = sem("rope_done")
        rope_rest = sem("rope_rest")
        v_placed = [sem("v_plain"), sem("v_rope")]
        qk_landed = [[sem(f"qk{a}{g}") for g in range(2)] for a in range(2)]
        scored = sem("scored")
        max_taken = sem("max_taken")
        max_hi = sem("max_hi")
        max_r = sem("max_r")
        max_mid = sem("max_mid")
        max_split = sem("max_split")
        max_landed = [sem("max_plain"), sem("max_rope")]
        shifted = sem("shifted")
        weighed = sem("weighed")
        clip_dve = sem("clip_dve")
        clip_pool = sem("clip_pool")
        valued = sem("valued")
        o_copied = sem("o_copied")
        den_done = sem("den_done")
        inv_done = sem("inv_done")
        res_landed = sem("res_landed")
        res_moved = sem("res_moved")
        squared = sem("squared")
        summed = sem("summed")
        mean_done = sem("mean_done")
        rms_done = sem("rms_done")
        x1_done = sem("x1_done")
        route = sem("route")
        top_done = sem("top_done")
        z_exp = sem("z_exp")
        shares_done = sem("shares_done")
        tanh_done = sem("tanh_done")
        mixed = sem("mixed")
        scaled = sem("scaled")
        final_done = sem("final_done")
        stored = sem("stored")
        side_full = [sem("side_full0"), sem("side_full1")]
        side_free = [sem("side_free0"), sem("side_free1")]

        FIRST_LOADS = ((const_sb[:, 0:128], consts[:, 0:128]), (wq_sb[:], wq))
        LOADS = ((wkcT_sb, wkcT), (wk_sb, wk), (wvcT_sb, wvcT), (wvr_sb, wvr), (const_sb[:, 128:], consts[:, 128:]),
                 (wv_sb[:, 0, :], wvp), (wo_sb[:], wo), (w_up_sb[:], w_up),
                 (w_out_sb[:], w_out), (w2_sb[:], w2), (w_gate_sb[:], w_gate),
                 (bias_sb[:], bias[0].partition_broadcast(128)), (norm_sb[:], norms[0].partition_broadcast(128)))
        READY = 1 + EPG + 2
        ONES = 3 * 2
        ROUTE_A, ROUTE_B = 9, 19
        QK_ALL = 16 * QK_DMAS

        def stand(eng):
            eng.sem_inc(passed, 1)

        def full(eng, b, job):
            eng.wait_ge(side_full[side_bank(job)], side_uses(b, job) + 1)

        def free(job):
            return side_free[side_bank(job)]

        def taken(eng, b, job):
            if live(b, LAG[job]):
                eng.wait_ge(side_free[side_bank(job)], side_uses(b, job) + 1)

        def bank(job):
            return side_ps[:, side_bank(job), :]

        def tiles(ap):
            return ap.rearrange("p (t c) -> p t c", t=NT)

        def norms_done(b, lag, which):
            if isinstance(b, int):
                n = sum(live(c, -3) + live(c, -1) for c in range(-1, b))
                return n + (live(b, -3) if which == 0 else 0)
            head = sum(live(c, -3) + live(c, -1) for c in range(-1, FIRST_LOOP))
            return (b + (-FIRST_LOOP)) * 2 + (head + (1 if which == 0 else 0))

        def all_steps(eng, even, odd, after_first=None):
            for b in range(-1, FIRST_LOOP):
                even(b)
                odd(b)
                if b == -1 and after_first:
                    after_first()
            with eng.Fori(FIRST_LOOP, LAST_LOOP + 1) as b:
                even(b)
                odd(b)
            for b in range(LAST_LOOP + 1, B + 3):
                even(b)
                odd(b)

        block = ctx.enter_context(nc.Block())

        @block.sync
        def _(sp):
            sp.dma_start(x_in[:], x[0]).then_inc(x_landed, 16)
            for dst, src in FIRST_LOADS:
                sp.dma_start(dst, src).then_inc(loaded_first, 16)
            for dst, src in LOADS:
                sp.dma_start(dst, src).then_inc(loaded, 16)
            sp.wait_ge(kt_zeroed, 2)

            def hold(semaphore, value):
                if not isinstance(value, int) or value > 0:
                    sp.wait_ge(semaphore, value)
                    stand(sp)

            def place_qk(b, lag, a, gh):
                if not live(b, lag):
                    return
                for s in (hi_done[a], mid_done[a], lo_done[a]):
                    hold(s, cnt(b, lag, 2, 2))
                if not isinstance(b, int) or b + lag > 0:
                    hold(shifted, cnt(b, lag - 1, 2 * UNIT, UNIT * a + UNIT // 2 * (gh + 1)))
                for t in range(TERMS):
                    sp.dma_start(qt[a][16 * t:16 * t + 16, 4 * gh:4 * gh + 4, :],
                                 q_parts[a][64 * gh:64 * gh + 64, Q_PART[t], :]).then_inc(qk_landed[a][gh], 16)
                    for ab in range(2):
                        row, i, p = 16 * t + 8 * ab, 8 * gh + 4 * ab, 64 * gh + 32 * ab
                        sp.dma_start(kt[a][row:row + 8, i:i + 4, :],
                                     k_parts[a][p:p + 32, K_PART[t], :]).then_inc(qk_landed[a][gh], 16)

            def place_max(b, job):
                lag, a, gh = LAG[job], int(job[4:-1] == "rope"), int(job[-1])
                if live(b, lag):
                    taken(sp, b, job)
                    stand(sp)
                    sp.dma_start(qt[a][ROWS:ROWS + MROWS, 4 * gh:4 * gh + 4, :],
                                 max_rows[:, gh, :]).then_inc(max_landed[a], 16)

            def even(b):
                place_qk(b, 0, PLAIN, 1)
                place_max(b, "max_rope1")
                if live(b, -1):
                    taken(sp, b + (-1), "y_rope")
                    stand(sp)
                    hold(mid_landed, cnt(b, -1, 16, 16))
                    sp.dma_start(xn_old[:], xn_mid[:]).then_inc(old_landed, 16)
                if live(b, 0):
                    hold(old_landed, cnt(b, -1, 16, 16))
                    hold(xn_done, cnt(b, 0, NT, NT))
                    sp.dma_start(xn_mid[:], xn_new[:]).then_inc(mid_landed, 16)
                if live(b, 1) and live(b, 0):
                    hold(xn_done, cnt(b, 1, NT, 0))
                    sp.dma_start(x_in[:], x[b + 1]).then_inc(x_landed, 16)
                if live(b, -3):
                    hold(final_done, cnt(b, -3, 1, 1))
                    sp.dma_start(out[b + (-3)], out_sb[:]).then_inc(stored, 16)
                if live(b, -2):
                    hold(final_done, cnt(b, -2, 1, 0))
                    taken(sp, b + (-1), "y_plain")
                    stand(sp)
                    sp.dma_start(res_old[:], res_new[:]).then_inc(res_moved, 16)
                if live(b, -1):
                    hold(res_moved, cnt(b, -1, 16, 0))
                    sp.dma_start(res_new[:], x[b + (-1)]).then_inc(res_landed, 16)
                place_qk(b, 0, ROPE, 0)
                place_max(b, "max_plain0")

            def odd(b):
                place_qk(b, 0, ROPE, 1)
                place_max(b, "max_plain1")
                place_qk(b, 1, PLAIN, 0)
                place_max(b, "max_rope0")

            all_steps(sp, even, odd)
            sp.wait_ge(stored, 16 * B)

        @block.tensor
        def _(pe):
            pe.wait_ge(loaded_first, 16 * len(FIRST_LOADS))

            def merge_weights():
                pe.wait_ge(loaded, 16 * len(LOADS))
                to = o_ps[:, :]
                pe.matmul(to[:, 0:128], wkcT_sb[:, :], wk_sb[:, 0, :], start=True, stop=True)
                pe.matmul(to[:, 128:256], wkcT_sb[:, :], wk_sb[:, 1, :], start=True, stop=True)
                pe.matmul(to[:, 256:384], wvcT_sb[:, :], wvr_sb[:, :], start=True, stop=True).then_inc(product, 1)
                pe.wait_ge(merged, 3)

            def score(b, a, t):
                if not live(b, 0):
                    return
                i, tile = t // 4, t % 4
                if i % 8 == 0 and tile == 0:
                    pe.wait_ge(qk_landed[a][i // 8], cnt(b, 0, QK_ALL, QK_ALL))
                last = (-1, 0, -2)[t] if a == PLAIN and t < 3 else t - 2
                need(pe, max_taken, cnt(b, 0, 2 * UNIT, UNIT * a + last))
                pe.matmul(score_ps[:, score_bank(a, t), :],
                          qt[a][0:ROWS, 4 * (i // 8) + i % 4, 128 * tile:128 * tile + 128],
                          kt[a][0:ROWS, i, :], start=True, stop=True).then_inc(scored, 1)

            def shift(b, lag, a, t):
                if not live(b, lag):
                    return
                i, tile = t // 4, t % 4
                if isinstance(b, int) and b == 0 and a == PLAIN and t == 0:
                    pe.wait_ge(kt_ones, ONES)
                if i % 8 == 0 and tile == 0:
                    pe.wait_ge(max_landed[a], cnt(b, lag, 32, 16 * (i // 8 + 1)))
                need(pe, weighed, cnt(b, lag, 2 * UNIT, UNIT * a + t - 1))
                pe.matmul(shift_ps[:, t % 2, :], kt[a][:, i, 128 * tile:128 * tile + 128],
                          qt[a][:, 4 * (i // 8) + i % 4, :], start=True, stop=True).then_inc(shifted, 1)

            def value(b, lag, a, quad, tile):
                if not live(b, lag):
                    return
                if tile == 0:
                    if a == PLAIN:
                        pe.wait_ge(clip_dve, cnt(b, lag, 24, 6 * quad + 6))
                        pe.wait_ge(clip_pool, cnt(b, lag, 4, quad + 1))
                    else:
                        pe.wait_ge(weighed, cnt(b, lag, 2 * UNIT, UNIT + 16 * (quad + 1)))
                    if quad == 0:
                        pe.wait_ge(v_placed[a], cnt(b, lag, 2, 4))
                    if quad % 2 == 0:
                        need(pe, o_copied, cnt(b, lag, 4, 2 * a + quad // 2))
                ab = quad % 2
                for j in range(4):
                    mm = pe.matmul(o_ps[32 * j:32 * j + 32, :],
                                   vt[a][:, tile, 4 * (quad // 2) + j, 16 * ab:16 * ab + 32],
                                   weights[:, 4 * (quad % 2) + j, tile, :],
                                   start=(ab == 0 and tile == 0), stop=(ab == 1 and tile == 3))
                mm.then_inc(valued, 1)

            def side(b, job, part):
                lag = LAG[job]
                if not live(b, lag):
                    return
                to, at = bank(job), side_bank(job)
                if part == 0:
                    need(pe, side_free[at], side_uses(b, job))

                def turn(src, n=128):
                    for tile in range(NT):
                        mm = pe.transpose(to[0:n, 128 * tile:128 * tile + 128], src(tile), ident)
                    mm.then_inc(side_full[at], 1)

                if job[:4] == "max_":
                    a, gh = int(job[4:-1] == "rope"), int(job[-1])
                    pe.wait_ge(max_split, cnt(b, lag, 4, 2 * a + gh + 1))
                    for tile in range(NT):
                        mm = pe.transpose(to.bitcast(BF16)[0:24, 128 * tile:128 * tile + 128],
                                          max_parts[:, gh, tile, :], ident_bf[:, :])
                    mm.then_inc(side_full[at], 1)
                elif job[:2] == "o_":
                    a, gh = int(job[2:-1] == "rope"), int(job[-1])
                    pe.wait_ge(o_copied, cnt(b, lag, 4, 2 * a + gh + 1))
                    turn(lambda tile: o_sb[:, 128 * tile:128 * tile + 128])
                elif job[:4] == "back":
                    a = int(job == "back_rope")
                    taken(pe, b, ("o_plain1", "o_rope1")[a])
                    turn(lambda tile: heads[a][:, tile, :])
                elif job[:2] == "y_":
                    a = int(job == "y_rope")
                    taken(pe, b, ("back_plain", "back_rope")[a])
                    for tile in range(NT):
                        mm = pe.matmul(to[:, 128 * tile:128 * tile + 128], headsT[:, 128 * tile:128 * tile + 128],
                                       wo_sb[:, a, :], start=True, stop=True)
                    mm.then_inc(side_full[at], 1)
                elif job == "xnT":
                    pe.wait_ge(xn_done, cnt(b, lag, NT, NT))
                    turn(lambda tile: xn_new[:, tile, :])
                elif job in ("q_plain", "k_plain", "q_rope", "qs_rope", "k_rope", "ks_rope"):
                    if job[1:] == "_plain":
                        taken(pe, b, "xnT")
                    w = {"q_plain": wq_sb[:, 0, :], "k_plain": wq_sb[:, 1, :], "q_rope": wq_sb[:, 2, :],
                         "qs_rope": wq_sb[:, 3, :], "k_rope": wkr_sb[:, 0, :], "ks_rope": wkr_sb[:, 1, :]}[job]
                    pe.matmul(to, w, xnT[:, :], start=True, stop=True).then_inc(side_full[at], 1)
                elif job in ("v0", "v1"):
                    for j in range(2):
                        tile = 2 * int(job[1]) + j
                        mm = pe.matmul(to[:, 256 * j:256 * j + 256], xnT[:, 128 * tile:128 * tile + 128],
                                       wv_sb[:, :, :].rearrange("p a c -> p (a c)"), start=True, stop=True)
                    mm.then_inc(side_full[at], 1)
                elif job == "x1T":
                    pe.wait_ge(x1_done, cnt(b, lag, NT, NT))
                    turn(lambda tile: x1[:, tile, :])
                elif job == "gates":
                    taken(pe, b, "x1T")
                    for tile in range(NT):
                        mm = pe.matmul(to[:, NL * tile:NL * tile + NL], x1T[:, 128 * tile:128 * tile + 128],
                                       w_gate_sb[:, :], start=True, stop=True)
                    mm.then_inc(side_full[at], 1)
                elif job[:2] == "up" or job[:4] == "down":
                    w = 2 * int(job[-1]) + int(job[0] == "d")
                    pe.matmul(to, w_up_sb[:, w, :], x1T[:, :], start=True, stop=True).then_inc(side_full[at], 1)
                elif job == "shared_out":
                    taken(pe, b, "down3")
                    for tile in (2 * part, 2 * part + 1):
                        for c in range(2):
                            mm = pe.matmul(to[:, 128 * tile:128 * tile + 128],
                                           hidden[:, c, 128 * tile:128 * tile + 128], w_out_sb[:, c, :],
                                           start=(c == 0), stop=(c == 1))
                    if part == 1:
                        mm.then_inc(side_full[at], 1)
                else:
                    n = int(job[3:])
                    tile, e = n // 2, n % 2
                    mm = pe.matmul(to, hidden[:, 2 + part, 128 * tile:128 * tile + 128],
                                   w2_sb[:, part, 512 * e:512 * e + 512], start=(part == 0), stop=(part == 1))
                    if part == 1:
                        mm.then_inc(side_full[at], 1)

            def step(b, which):
                for t in range(UNIT):
                    i = t // 4
                    unit, k = divmod(i + 11, 16)
                    if which == "even":
                        score(b, PLAIN, t)
                        shift(b, -1, ROPE, t)
                        if t % 4 == VALUE_AT:
                            value(b, -1, (PLAIN, ROPE)[unit], k // 4, k % 4)
                    else:
                        score(b, ROPE, t)
                        shift(b, 0, PLAIN, t)
                        if t % 4 == VALUE_AT:
                            value(b, unit - 1, (ROPE, PLAIN)[unit], k // 4, k % 4)
                    for job, part in jobs_at(which, t):
                        side(b, job, part)

            all_steps(pe, lambda b: step(b, "even"), lambda b: step(b, "odd"), merge_weights)

        @block.scalar
        def _(act):
            def weigh(b, lag, a, t):
                if not live(b, lag):
                    return
                i, tile = t // 4, t % 4
                if i % 4 == 0:
                    need(act, valued, cnt(b, lag, 32, 16 * a + 4 * (i // 4) - 7 + tile))
                act.wait_ge(shifted, cnt(b, lag, 2 * UNIT, UNIT * a + t + 1))
                act.activation(weights[:, i % 8, tile, :], shift_ps[:, t % 2, :], ACT.Exp,
                               scale=SCALE).then_inc(weighed, 1)

            def copy_max(b, job):
                lag, a, gh = LAG[job], int(job[4:-1] == "rope"), int(job[-1])
                if live(b, lag):
                    full(act, b, job)
                    need(act, max_landed[1 - a], cnt(b, lag + a - 1, 32, 16 * (gh + 1)))
                    act.activation(max_rows[:, gh, :], bank(job).bitcast(BF16)[0:24, 0:S],
                                   ACT.Copy).then_inc(free(job), 1)

            def copy_o(b, job, before, lag_before):
                lag, a, gh = LAG[job], int(job[2:-1] == "rope"), int(job[-1])
                if live(b, lag):
                    act.wait_ge(valued, cnt(b, lag, 32, 16 * a + 8 * (gh + 1)))
                    if live(b, lag_before + LAG[before]):
                        full(act, b + lag_before, before)
                    act.activation(o_sb[:, :], o_ps[:, :], ACT.Copy).then_inc(o_copied, 1)

            def copy_side(b, job, dst):
                if live(b, LAG[job]):
                    full(act, b, job)
                    act.activation(dst, bank(job), ACT.Copy).then_inc(free(job), 1)

            def weight_experts(b, n):
                if live(b, -2):
                    full(act, b, f"exp{n}")
                    act.wait_ge(route, cnt(b, -2, ROUTE_A + ROUTE_B, ROUTE_A + ROUTE_B))
                    if n >= 2:
                        act.wait_ge(mixed, cnt(b, -2, 24, 3 * (n - 2) + 1))
                    for e in range(4):
                        last = act.activation(spread[:, n % 2, e, :], bank(f"exp{n}")[:, 128 * e:128 * e + 128],
                                              ACT.Copy, scale=gate[:, n // 2, 4 * (n % 2) + e:4 * (n % 2) + e + 1])
                    last.then_inc(free(f"exp{n}"), 1)

            def part(b, lag, t, job, quarter, a, src, parts, hi):
                if t == quarter and live(b, lag):
                    which = int(job[0] == "k")
                    if hi and a == PLAIN:
                        full(act, b, job)
                    elif hi:
                        act.wait_ge(rope_done, cnt(b, lag, 2, 1 + which))
                    if hi:
                        for gh in range(2):
                            need(act, qk_landed[a][gh], cnt(b, lag, QK_ALL, 0))
                        act.activation(parts[a][:, 0, :], src, ACT.Copy).then_inc(hi_done[a], 1)
                    else:
                        if a == PLAIN:
                            taken(act, b, job)
                        else:
                            act.wait_ge(rope_rest, cnt(b, lag, 2, 1 + which))
                        act.activation(parts[a][:, 1, :], src, ACT.Copy).then_inc(mid_done[a], 1)

            def even(b):
                for t in range(UNIT):
                    weigh(b, -1, ROPE, t)
                    if t == after("even", "x1T"):
                        copy_side(b, "x1T", x1T[:, :])
                    if t == after("even", "max_rope1"):
                        copy_max(b, "max_rope1")
                    part(b, 0, t, "q_rope", after("even", "qs_rope", 3), ROPE, roped[:, 0, :], q_parts, True)
                    part(b, 0, t, "k_rope", after("even", "ks_rope", 3), ROPE, roped[:, 1, :], k_parts, True)
                    for n in range(4):
                        if t == after("even", f"up{n}") and live(b, -2):
                            full(act, b, f"up{n}")
                            if n:
                                taken(act, b, f"up{n - 1}")
                            act.activation(tanh[:, :], bank(f"up{n}"), ACT.Tanh, scale=0.5).then_inc(tanh_done, 1)
                    if t == 18:
                        copy_o(b, "o_plain1", "o_plain0", -1)
                    part(b, 0, t, "q_rope", after("even", "qs_rope", 10), ROPE, q_rest[:, :], q_parts, False)
                    part(b, 0, t, "k_rope", after("even", "ks_rope", 8), ROPE, k_rest[:, :], k_parts, False)
                    if t == after("even", "back_plain"):
                        copy_side(b, "back_plain", headsT[:, :])
                    if t == after("even", "max_plain0"):
                        copy_max(b, "max_plain0")
                    if t == 47 and live(b, -2):
                        act.wait_ge(route, cnt(b, -2, ROUTE_A + ROUTE_B, ROUTE_A))
                        act.activation(ez[:], z[:], ACT.Exp).then_inc(z_exp, 1)
                    if t == 50:
                        copy_o(b, "o_rope0", "o_plain1", 0)
                    for n in range(2):
                        if t == after("even", f"v{n}", 1) and live(b, 0):
                            for a in range(2):
                                need(act, v_placed[a], cnt(b, 0, 2, 2))
                            copy_side(b, f"v{n}", v_stage[:, 2 * n:2 * n + 2, :, :].rearrange("p t a c -> p (t a c)"))

            def odd(b):
                for t in range(UNIT):
                    weigh(b, 0, PLAIN, t)
                    if t == after("odd", "max_plain1"):
                        copy_max(b, "max_plain1")
                    if t == after("odd", "xnT"):
                        copy_side(b, "xnT", xnT[:, :])
                    part(b, 1, t, "q_plain", after("odd", "q_plain"), PLAIN, bank("q_plain"), q_parts, True)
                    part(b, 1, t, "q_plain", after("odd", "q_plain", 3), PLAIN, q_rest[:, :], q_parts, False)
                    part(b, 1, t, "k_plain", after("odd", "k_plain"), PLAIN, bank("k_plain"), k_parts, True)
                    part(b, 1, t, "k_plain", after("odd", "k_plain", 4), PLAIN, k_rest[:, :], k_parts, False)
                    for n in range(8):
                        if t == after("odd", f"exp{n}"):
                            weight_experts(b, n)
                    if t == 18:
                        copy_o(b, "o_rope1", "o_rope0", 0)
                    if t == after("odd", "back_rope"):
                        copy_side(b, "back_rope", headsT[:, :])
                    if t == after("odd", "max_rope0"):
                        copy_max(b, "max_rope0")
                    if t == 50:
                        copy_o(b, "o_plain0", "o_rope1", 0)

            all_steps(act, even, odd)

        @block.vector
        def _(dve):
            dve.memset(kt[PLAIN][:, :, :].bitcast(F32), 0.0).then_inc(kt_zeroed, 1)

            def constants():
                pair = float(np.array([0x3F803F80], np.uint32).view(np.float32)[0])
                own = [kt[a][:, :, :].bitcast(F32).rearrange("p (g ab c) n -> p g ab c n", g=2, ab=2)
                       for a in range(2)]
                dve.wait_ge(kt_zeroed, 2)
                for a in range(2):
                    dve.memset(own[a][ROWS:ROWS + 3, :, 0], pair).then_inc(kt_ones, 1)
                    dve.memset(own[a][ROWS:ROWS + 6, :, 1], pair).then_inc(kt_ones, 1)
                dve.wait_ge(kt_ones, 4)
                for a in range(2):
                    dve.memset(own[a][ROWS:ROWS + 3, :, 1], 0.0).then_inc(kt_ones, 1)
                dve.wait_ge(loaded, 16 * len(LOADS))
                dve.tensor_copy(ident_bf[:, :], ident).then_inc(merged, 1)
                dve.wait_ge(product, 1)
                dve.tensor_copy(wkr_sb[:, :, :].rearrange("p a c -> p (a c)"), o_ps[:, 0:256]).then_inc(merged, 1)
                dve.tensor_copy(wv_sb[:, 1, :], o_ps[:, 256:384]).then_inc(merged, 1)

            def maximum(b, a, t):
                if not live(b, 0):
                    return
                i, tile = t // 4, t % 4
                if t % 32 == 0:
                    need(dve, max_split, cnt(b, 0, 4, 2 * a + i // 8 - 1))
                dve.wait_ge(scored, cnt(b, 0, 2 * UNIT, UNIT * a + t + 1))
                dve.tensor_reduce(negmax[:, i // 8, tile, i % 8:i % 8 + 1], score_ps[:, score_bank(a, t), :], AX.X, ALU.max,
                                  negate=True).then_inc(max_taken, 1)

            def clip(b, lag, i, part):
                if live(b, lag):
                    dve.wait_ge(weighed, cnt(b, lag, 2 * UNIT, NT * i + 2 * part + 2))
                    half = weights[:, i % 8, 2 * part:2 * part + 2]
                    dve.tensor_scalar(half, half, FLOOR, None, ALU.max).then_inc(clip_dve, 1)

            def normalise(b, job):
                lag, a, gh = LAG[job], int(job[2:-1] == "rope"), int(job[-1])
                if not live(b, lag):
                    return
                full(dve, b, job)
                o = bank(job).rearrange("p (t h c) -> p t h c", t=NT, h=8)
                dve.tensor_scalar(den[:], o[:, :, :, DH], EPS_DEN if a == PLAIN else 0.0, None,
                                  ALU.add).then_inc(den_done, 1)
                dve.wait_ge(den_done, cnt(b, lag, 4, 2 * a + gh + 1))
                dve.reciprocal(inv_den[:], den[:]).then_inc(inv_done, 1)
                dve.wait_ge(inv_done, cnt(b, lag, 4, 2 * a + gh + 1))
                dve.tensor_tensor(heads[a][:, :, 64 * gh:64 * gh + 64].rearrange("p t (h c) -> p t h c", h=8),
                                  o[:, :, :, 0:DH], inv_den[:].unsqueeze(3).broadcast_to([128, NT, 8, DH]),
                                  ALU.mult).then_inc(free(job), 1)

            def add_side(b, job, dst, other):
                full(dve, b, job)
                dve.tensor_tensor(dst, tiles(bank(job)), other, ALU.add).then_inc(free(job), 1)

            def scale(b, dst, src, which, lag, signal):
                dve.wait_ge(rms_done, norms_done(b, lag, which) + 1)
                for tile in range(NT):
                    dve.scalar_tensor_tensor(out=dst[:, tile, :], in0=src[:, tile, :],
                                             scalar=rms[:, which, tile:tile + 1], in1=norm_sb[:, which, :],
                                             op0=ALU.mult, op1=ALU.mult).then_inc(signal, 1)

            def mean_square(b, which, lag):
                dve.wait_ge(squared, norms_done(b, lag, which) + 1)
                dve.tensor_reduce(sums[:, which, :], square, AX.X, ALU.add).then_inc(summed, 1)

            def even(b):
                for t in range(UNIT):
                    maximum(b, PLAIN, t)
                    if t in (1, 2):
                        clip(b, -1, H - 1, t - 1)
                    if t == 4 and live(b, -3):
                        mean_square(b, 1, -3)
                    if t == 7 and live(b, -3):
                        scale(b, out_sb, out_sb, 1, -3, scaled)
                    if t == after("even", "gates") and live(b, -2):
                        full(dve, b, "gates")
                        dve.tensor_tensor(logits[:], bank("gates")[:, 0:NT * NL].rearrange("p (t l) -> p t l", t=NT),
                                          bias_sb[:, :].unsqueeze(1).broadcast_to([128, NT, NL]),
                                          ALU.add).then_inc(free("gates"), 1)
                    for job, dst, table in (("q_rope", roped[:, 0, :], cos), ("qs_rope", turned[:, :], sin),
                                            ("k_rope", roped[:, 1, :], cos), ("ks_rope", turned[:, :], sin)):
                        if t == after("even", job) and live(b, 0):
                            full(dve, b, job)
                            need(dve, rope_rest, cnt(b, 0, 2, 0))
                            if job == "ks_rope":
                                dve.wait_ge(rope_done, cnt(b, 0, 2, 1))
                            dve.tensor_tensor(dst, bank(job), table, ALU.mult).then_inc(free(job), 1)
                    for n in range(4):
                        if t == after("even", f"up{n}", 2) and live(b, -2):
                            dve.wait_ge(tanh_done, cnt(b, -2, 4, n + 1))
                            dve.scalar_tensor_tensor(out=hidden[:, n, :], in0=tanh[:, :], scalar=1.0,
                                                     in1=bank(f"up{n}"), op0=ALU.add,
                                                     op1=ALU.mult).then_inc(free(f"up{n}"), 1)
                        if t == after("even", f"down{n}", 1) and live(b, -2):
                            full(dve, b, f"down{n}")
                            taken(dve, b, f"up{n}")
                            dve.scalar_tensor_tensor(out=hidden[:, n, :], in0=hidden[:, n, :], scalar=0.5,
                                                     in1=bank(f"down{n}"), op0=ALU.mult,
                                                     op1=ALU.mult).then_inc(free(f"down{n}"), 1)
                    if t == after("even", "o_plain1"):
                        normalise(b, "o_plain1")
                    if t == after("even", "y_plain") and live(b, -1):
                        dve.wait_ge(res_landed, cnt(b, -1, 16, 16))
                        add_side(b, "y_plain", res_new[:], res_new[:])
                    if t == 44 and live(b, -2):
                        dve.wait_ge(route, cnt(b, -2, ROUTE_A + ROUTE_B, ROUTE_A - 1))
                        dve.tensor_reduce(top[:], sel0[:], AX.X, ALU.max).then_inc(top_done, 1)
                    if t == 47 and live(b, -2):
                        dve.wait_ge(z_exp, cnt(b, -2, 1, 1))
                        dve.tensor_scalar(total[:, :, 0:1], ez[:, :, 0:1], 1.0, None, ALU.add).then_inc(shares_done, 1)
                        dve.tensor_reduce(total[:, :, 1:2], ez[:, :, 1:], AX.X, ALU.add).then_inc(shares_done, 1)
                        dve.wait_ge(shares_done, cnt(b, -2, 3, 2))
                        dve.reciprocal(share[:], total[:]).then_inc(shares_done, 1)
                    if t == after("even", "o_rope0"):
                        normalise(b, "o_rope0")
                    if t == 49 and live(b, 1):
                        dve.wait_ge(x_landed, cnt(b, 1, 16, 16))
                        need(dve, rstd_done, cnt(b, 1, 1, 0))
                        for tile in range(NT):
                            dve.bn_stats(stats[:, tile, :], x_in[:, tile, :]).then_inc(stats_done, 1)
                    if t == 50 and live(b, 1):
                        dve.wait_ge(stats_done, cnt(b, 1, NT, NT))
                        stand(dve)
                        for tile in range(NT):
                            dve.bn_aggr(moments[:, tile, :], stats[:, tile, :]).then_inc(moments_done, 1)
                    if t == 61 and live(b, 1):
                        dve.wait_ge(rstd_done, cnt(b, 1, 1, 1))
                        need(dve, mid_landed, cnt(b, 1, 16, 0))
                        for tile in range(NT):
                            dve.tensor_scalar(xn_new[:, tile, :], x_in[:, tile, :], moments[:, tile, 0:1],
                                              ln_rstd[:, tile:tile + 1], ALU.subtract, ALU.mult).then_inc(xn_done, 1)

            def odd(b):
                for t in range(UNIT):
                    maximum(b, ROPE, t)
                    if t % 4 in (1, 2) and t > 4 and (t // 4 - 1) % 4:
                        clip(b, 0, t // 4 - 1, t % 4 - 1)
                    for job, rest, quarter in (("q_plain", q_rest, 6), ("k_plain", k_rest, 12)):
                        if t == quarter and live(b, 1):
                            dve.wait_ge(hi_done[PLAIN], cnt(b, 1, 2, 1 + int(job[0] == "k")))
                            need(dve, mid_done[ROPE], cnt(b, 1, 2, 0))
                            need(dve, lo_done[ROPE], cnt(b, 1, 2, 0))
                            parts = q_parts if job[0] == "q" else k_parts
                            dve.tensor_tensor(rest[:, :], bank(job), parts[PLAIN][:, 0, :],
                                              ALU.subtract).then_inc(free(job), 1)
                    if t == after("odd", "shared_out") and live(b, -2):
                        need(dve, stored, cnt(b, -2, 16, 0))
                        add_side(b, "shared_out", out_sb[:], x1[:])
                    if t == after("odd", "o_rope1"):
                        normalise(b, "o_rope1")
                    if t == after("odd", "y_rope") and live(b, -1):
                        dve.wait_ge(old_landed, cnt(b, -1, 16, 16))
                        taken(dve, b, "shared_out")
                        add_side(b, "y_rope", x1[:], xn_old[:])
                    if t == 29 and live(b, -1):
                        mean_square(b, 0, -1)
                    if t == 40 and live(b, -1):
                        scale(b, x1, x1, 0, -1, x1_done)
                    if t == after("odd", "o_plain0"):
                        normalise(b, "o_plain0")

            all_steps(dve, even, odd, constants)

        @block.gpsimd
        def _(pool):
            pool.memset(minus_half[:, :], -0.5).then_inc(ready, 1)
            pool.memset(kt[ROPE][:, :, :].bitcast(F32), 0.0).then_inc(kt_zeroed, 1)
            pool.wait_ge(kt_zeroed, 2)
            pool.wait_ge(ready, 1)

            def constants():
                for e in range(EPG):
                    pool.memset(rank0[:, :, e:e + 1], float(EPG - 1 - e)).then_inc(ready, 1)
                for a in range(2):
                    pool.memset(vt[a][:], 0.0).then_inc(ready, 1)
                pool.wait_ge(ready, READY)
                for a in range(2):
                    for ab in range(2):
                        pool.memset(vt[a][:, :, :, 32 * ab + DH:32 * ab + DH + 1], 1.0).then_inc(v_placed[a], 1)

            def split_max(b, job):
                lag, a, gh = LAG[job], int(job[4:-1] == "rope"), int(job[-1])
                if not live(b, lag):
                    return
                n = cnt(b, lag, 4, 2 * a + gh + 1)

                def part(k):
                    return max_parts[:, gh].rearrange("p t (ab k g) -> p t ab k g", ab=2, k=3)[:, :, :, k, :]

                def heads_of(ap):
                    return ap.rearrange("p t (ab g) -> p t ab g", ab=2)

                pool.wait_ge(max_taken, cnt(b, lag, 2 * UNIT, UNIT * a + 32 * (gh + 1)))
                stand(pool)
                pool.tensor_copy(part(0), heads_of(negmax[:, gh])).then_inc(max_hi, 1)
                pool.wait_ge(max_hi, n)
                pool.tensor_tensor(heads_of(max_rest[:]), heads_of(negmax[:, gh]), part(0), ALU.subtract)\
                    .then_inc(max_r, 1)
                pool.wait_ge(max_r, n)
                stand(pool)
                pool.tensor_copy(part(1), heads_of(max_rest[:])).then_inc(max_mid, 1)
                pool.wait_ge(max_mid, n)
                pool.tensor_tensor(part(2), heads_of(max_rest[:]), part(1), ALU.subtract).then_inc(max_split, 1)

            def place_v(b, a):
                if not live(b, 0):
                    return
                taken(pool, b, "v1")
                need(pool, valued, cnt(b, -1, 32, 16 * (a + 1)))
                stand(pool)
                for ab in range(2):
                    src = v_stage[:, :, a, :].rearrange("p t (h ab c) -> p t h ab c", ab=2, c=DH)[:, :, :, ab, :]
                    pool.tensor_copy(vt[a][:, :, :, 32 * ab:32 * ab + DH], src).then_inc(v_placed[a], 1)

            def root(b, lag, which):
                pool.wait_ge(summed, norms_done(b, lag, which) + 1)
                stand(pool)
                pool.tensor_scalar(sums[:, which, :], sums[:, which, :], 1.0 / D, EPS_RMS, ALU.mult,
                                   ALU.add).then_inc(mean_done, 1)
                pool.wait_ge(mean_done, norms_done(b, lag, which) + 1)
                pool.tensor_tensor(rms[:, which, :], sums[:, which, :], minus_half[:, :], ALU.pow).then_inc(rms_done, 1)

            def clip(b, i):
                if live(b, 0):
                    pool.wait_ge(weighed, cnt(b, 0, 2 * UNIT, NT * (i + 1)))
                    stand(pool)
                    pool.tensor_scalar(weights[:, i % 8], weights[:, i % 8], FLOOR, None, ALU.max).then_inc(clip_pool, 1)

            def router(b, first):
                k = [0 if first else ROUTE_A]
                base = lambda n: cnt(b, -2, ROUTE_A + ROUTE_B, n)

                def then(ins):
                    k[0] += 1
                    ins.then_inc(route, 1)
                    pool.wait_ge(route, base(k[0]))
                    stand(pool)

                def wide(ap, n):
                    return ap.broadcast_to([128, NT, n])

                tt = pool.tensor_tensor
                in0, in1 = in_group[:, 0], in_group[:, 1]
                le = logits[:, :, G:NL]
                if first:
                    taken(pool, b, "gates")
                    taken(pool, b + (-1), "exp7")
                    then(tt(gap[:], logits[:, :, 0:1], logits[:, :, 1:2], ALU.subtract))
                    then(pool.tensor_scalar(in0, gap[:], 0.0, None, ALU.is_ge))
                    then(pool.tensor_scalar(in1, in0, -1.0, 1.0, ALU.mult, ALU.add))
                    then(pool.tensor_scalar(low[:], gap[:], 0.0, 2.0, ALU.min, ALU.mult))
                    then(tt(z[:, :, 0:1], low[:], gap[:], ALU.subtract))
                    then(tt(sel0[:], le[:, :, 0:EPG], wide(in0, EPG), ALU.mult))
                    then(tt(sel1[:], le[:, :, EPG:E], wide(in1, EPG), ALU.mult))
                    then(tt(sel0[:], sel0[:], sel1[:], ALU.add))
                    pool.wait_ge(top_done, cnt(b, -2, 1, 1))
                    then(tt(z[:, :, 1:], sel0[:], wide(top[:], EPG), ALU.subtract))
                    assert k[0] == ROUTE_A
                    return
                pool.wait_ge(shares_done, cnt(b, -2, 3, 3))
                then(tt(prob[:], ez[:, :, 1:], wide(share[:, :, 1:2], EPG), ALU.mult))
                then(tt(prob[:], prob[:], wide(share[:, :, 0:1], EPG), ALU.mult))
                for s in range(1, EPG):
                    c, n = above[s - 1], EPG - s
                    then(tt(c[:], prob[:, :, 0:n], prob[:, :, s:EPG], ALU.subtract))
                    then(pool.tensor_scalar(c[:], c[:], 0.0, None, ALU.is_ge))
                    then(tt(rank[:, :, s:EPG], (rank0 if s == 1 else rank)[:, :, s:EPG], c[:], ALU.add))
                    if s == 1:
                        then(tt(rank[:, :, 0:1], rank0[:, :, 0:1], c[:, :, 0:1], ALU.subtract))
                        then(tt(rank[:, :, 1:n], rank[:, :, 1:n], c[:, :, 1:n], ALU.subtract))
                    else:
                        then(tt(rank[:, :, 0:n], rank[:, :, 0:n], c[:], ALU.subtract))
                then(pool.tensor_scalar(rank[:], rank[:], 1.5, None, ALU.is_lt))
                then(tt(prob[:], prob[:], rank[:], ALU.mult))
                then(tt(gate[:, :, 0:EPG], prob[:], wide(in0, EPG), ALU.mult))
                then(tt(gate[:, :, EPG:E], prob[:], wide(in1, EPG), ALU.mult))
                assert k[0] == ROUTE_A + ROUTE_B

            def mix(b, n):
                if live(b, -2):
                    taken(pool, b, f"exp{n}")
                    taken(pool, b, "shared_out")
                    pool.tensor_tensor(two[:], spread[:, n % 2, 0:2, :], spread[:, n % 2, 2:4, :],
                                       ALU.add).then_inc(mixed, 1)
                    pool.wait_ge(mixed, cnt(b, -2, 24, 3 * n + 1))
                    pool.tensor_tensor(one[:, :], two[:, 0, :], two[:, 1, :], ALU.add).then_inc(mixed, 1)
                    pool.wait_ge(mixed, cnt(b, -2, 24, 3 * n + 2))
                    pool.tensor_tensor(out_sb[:, n // 2, :], out_sb[:, n // 2, :], one[:, :], ALU.add).then_inc(mixed, 1)
                    pool.wait_ge(mixed, cnt(b, -2, 24, 3 * n + 3))

            def turn(b, n, last):
                if live(b, 0):
                    taken(pool, b, ("q_rope", "k_rope")[n])
                    taken(pool, b, last)
                    pool.tensor_tensor(roped[:, n, :], roped[:, n, :], turned[:, :], ALU.add).then_inc(rope_done, 1)

            def rope_less_first(b, n, rest, parts):
                if live(b, 0):
                    pool.wait_ge(hi_done[ROPE], cnt(b, 0, 2, n + 1))
                    pool.wait_ge(mid_done[PLAIN], cnt(b, 0, 2, 2))
                    pool.tensor_tensor(rest[:, :], roped[:, n, :], parts[ROPE][:, 0, :],
                                       ALU.subtract).then_inc(rope_rest, 1)

            def third(b, lag, a, n, rest, parts):
                if live(b, lag):
                    pool.wait_ge(mid_done[a], cnt(b, lag, 2, n + 1))
                    pool.tensor_tensor(parts[a][:, 2, :], rest[:, :], parts[a][:, 1, :],
                                       ALU.subtract).then_inc(lo_done[a], 1)

            def even(b):
                if live(b, -3):
                    pool.tensor_tensor(square, out_sb[:], out_sb[:], ALU.mult).then_inc(squared, 1)
                split_max(b, "max_rope1")
                if live(b, -3):
                    root(b, -3, 1)
                    pool.wait_ge(scaled, cnt(b, -3, NT, NT))
                    pool.wait_ge(res_moved, cnt(b, -3, 16, 16))
                    pool.tensor_tensor(out_sb[:], out_sb[:], res_old[:], ALU.add).then_inc(final_done, 1)
                turn(b, 0, "qs_rope")
                turn(b, 1, "ks_rope")
                rope_less_first(b, 0, q_rest, q_parts)
                rope_less_first(b, 1, k_rest, k_parts)
                third(b, 0, ROPE, 0, q_rest, q_parts)
                third(b, 0, ROPE, 1, k_rest, k_parts)
                split_max(b, "max_plain0")
                if live(b, -2):
                    router(b, True)
                if live(b, 1):
                    pool.wait_ge(moments_done, cnt(b, 1, NT, NT))
                    stand(pool)
                    pool.tensor_scalar(ln_var[:, :], moments[:, :, 1], EPS_LN, None, ALU.add).then_inc(var_done, 1)
                    pool.wait_ge(var_done, cnt(b, 1, 1, 1))
                    need(pool, xn_done, cnt(b, 1, NT, 0))
                    pool.tensor_tensor(ln_rstd[:, :], ln_var[:, :], minus_half[:, :], ALU.pow).then_inc(rstd_done, 1)
                if live(b, -2):
                    router(b, False)
                place_v(b, PLAIN)

            def odd(b):
                split_max(b, "max_plain1")
                clip(b, 0)
                third(b, 1, PLAIN, 0, q_rest, q_parts)
                third(b, 1, PLAIN, 1, k_rest, k_parts)
                place_v(b, ROPE)
                mix(b, 0)
                clip(b, 4)
                if live(b, -1):
                    taken(pool, b, "y_rope")
                    pool.tensor_tensor(square, x1[:], x1[:], ALU.mult).then_inc(squared, 1)
                    root(b, -1, 0)
                mix(b, 1)
                split_max(b, "max_rope0")
                mix(b, 2)
                clip(b, 8)
                mix(b, 3)
                mix(b, 4)
                mix(b, 5)
                mix(b, 6)
                clip(b, 12)
                mix(b, 7)

            all_steps(pool, even, odd, constants)


def kernel(**inputs):
    import concourse.bacc as _bacc
    from concourse.bass_utils import run_bass_kernel_spmd as _run

    g = {k.replace("L0_", ""): np.asarray(v) for k, v in inputs.items()}

    def in_order(w):
        return w.reshape(-1, 2, 4, 2, DH).transpose(0, 1, 3, 4, 2).reshape(-1, 128)

    def swapped(w):
        return w.reshape(-1, 64, 2)[:, :, ::-1].reshape(-1, 128)

    wqkv = g["attn_Wqkv"].T
    wq, wk = g["ffn_Wq"], g["ffn_Wk"]
    up = np.stack([g["ffn_W_shared_in"], g["ffn_W1_shared"]], 1).reshape(D, 2, 2, 2, 128)
    inv = (1.0 / 10000.0 ** (np.arange(0, DH, 2, dtype=np.float32) / DH)).astype(np.float32)
    ang = np.arange(S, dtype=np.float32)[:, None] * inv[None, :]
    sign = np.array([-1.0, 1.0] * (DH // 2), np.float32)
    by_d = [np.repeat(np.cos(ang), 2, 1).T, np.repeat(np.sin(ang), 2, 1).T * sign[:, None]]
    rows = [np.broadcast_to(t[None, :, None, :], (4, DH, 4, S)).reshape(128, S) for t in by_d]
    arrays = {
        "x": g["attn_x"].reshape(B, NT, 128, D).transpose(0, 2, 1, 3),
        "wq": np.stack([in_order(wqkv[:, 0:128]), in_order(wqkv[:, 128:256]), in_order(wq), in_order(swapped(wq))], 1),
        "wkcT": g["ffn_Wk_c"].T,
        "wk": np.stack([in_order(wk), in_order(swapped(wk))], 1),
        "wvcT": g["ffn_Wv_c"].T,
        "wvp": wqkv[:, 256:384],
        "wvr": g["ffn_Wv"],
        "wo": np.stack([g["attn_Wout"].T, g["ffn_Wo"]], 1),
        "w_up": up.transpose(0, 1, 3, 2, 4).reshape(D, 8, 128),
        "w_out": g["ffn_W_shared_out"].reshape(2, 128, D).transpose(1, 0, 2),
        "w2": g["ffn_W2_experts"].reshape(E, 2, 128, D).transpose(2, 1, 0, 3).reshape(128, 2, E * D),
        "w_gate": np.concatenate([g["ffn_Wg_gate"], g["ffn_We_gate"]], 1),
        "bias": np.concatenate([g["ffn_group_bias"], g["ffn_expert_bias"]])[None],
        "norms": np.stack([g["ffn_norm1_w"], g["ffn_norm2_w"]])[None],
        "consts": np.concatenate([np.eye(128, dtype=np.float32)] + rows, 1),
    }
    nc = _bacc.Bacc("TRN2", target_bir_lowering=False, num_devices=1, dynamic_dma_scratch_size=1024)
    feeds, aps = {}, {}
    for name, a in arrays.items():
        a = np.ascontiguousarray(a)
        feeds[f"in_{name}_dram"] = a
        aps[name] = nc.dram_tensor(f"in_{name}_dram", a.shape, mybir.dt.from_np(a.dtype), kind="ExternalInput").ap()
    out = nc.dram_tensor("out_0_dram", (B, 128, NT, D), F32, kind="ExternalOutput").ap()
    nc.disable_value_cache = True
    layer_kernel(nc, out=out, **aps)
    r = _run(nc, [feeds], core_ids=[0])
    y = r.results[0]["out_0_dram"]
    return y.reshape(B, 128, NT, D).transpose(0, 2, 1, 3).reshape(B, S, D)
```
